# Optimizing a Trainium2 kernel written in Bass

```python
import numpy as np
import jax
import jax.numpy as jnp

def _softmax(x, axis=-1):
    return jax.nn.softmax(x, axis=axis)

def _gelu(x):
    return jax.nn.gelu(x, approximate=True)

def _silu(x):
    return jax.nn.silu(x)

def _sigmoid(x):
    return jax.nn.sigmoid(x)

def _layernorm(x, axis=-1, eps=1e-05):
    m = jnp.mean(x, axis=axis, keepdims=True)
    v = jnp.var(x, axis=axis, keepdims=True)
    return (x - m) / jnp.sqrt(v + eps)

def _scatter_add(tgt, idx, src, axis=0):
    return tgt.at[idx].add(src)

def _segment_sum(src, seg, n):
    return jax.ops.segment_sum(src, seg, n)
kernel_name = 'mk_decoder_preln_d1_seqx_r4_0a4f2e'

def setup_inputs(seed: int=0):
    np.random.seed(seed)
    _w = jnp.asarray

    def _rec_inputs():
        import jax
        import jax.numpy as jnp
        _rk = jax.random.key(seed)
        x = -0.0003929 + 0.9999 * jax.random.normal(jax.random.fold_in(_rk, 1), (1, 2048, 256), jnp.float32)
        _lenS = 2048 - jax.random.randint(jax.random.fold_in(_rk, 7), (1,), 0, max(1, 2048 // 4) + 1, jnp.int32)
        _lenS2 = 1601 - jax.random.randint(jax.random.fold_in(_rk, 8), (1,), 0, max(1, 1601 // 4) + 1, jnp.int32)
        _ctx_2048P = jax.random.normal(jax.random.fold_in(_rk, 11), (1, 16, 512), jnp.float32)
        _ctx_2048c = jax.random.dirichlet(jax.random.fold_in(_rk, 511), 0.3 * jnp.ones((16,), jnp.float32), (1, 1601))
        _ctx_2048t = jnp.einsum('bsk,bkd->bsd', _ctx_2048c, _ctx_2048P)
        _ctx_2048t = _ctx_2048t * jax.lax.rsqrt(jnp.mean(jnp.square(_ctx_2048t)) + 1e-12) * 0.953939
        ctx_2048 = 4.13588e-05 + 0.999923 * (_ctx_2048t + 0.3 * jax.random.normal(jax.random.fold_in(_rk, 611), (1, 1601, 512), jnp.float32))
        _validS = jnp.arange(2048)[None, :] < _lenS[:, None]
        _validS2 = jnp.arange(1601)[None, :] < _lenS2[:, None]
        _causal = jnp.tril(jnp.ones((2048, 2048), dtype=bool))
        mask_BxS2_if0 = jnp.where(jnp.ones((1, 1601), dtype=bool), 4, 0).astype(jnp.int32)
        return (x, ctx_2048, mask_BxS2_if0)
    x, ctx_2048, mask_BxS2_if0 = _rec_inputs()

    def _L0_attn_setup():
        import jax, jax.numpy as jnp
        import numpy as np
        import math
        B, S, D_IN, D_KQ, D_OUT = (4, 512, 256, 256, 256)
        key = jax.random.key(seed)
        ks = jax.random.split(key, 7)
        sc = 0.02
        return {'x': jax.random.normal(ks[0], (B, S, D_IN), jnp.float32), 'Wq': jax.random.normal(ks[1], (D_KQ, D_IN), jnp.float32) * sc, 'bq': jax.random.normal(ks[2], (D_KQ,), jnp.float32) * sc, 'Wk': jax.random.normal(ks[3], (D_KQ, D_IN), jnp.float32) * sc, 'bk': jax.random.normal(ks[4], (D_KQ,), jnp.float32) * sc, 'Wv': jax.random.normal(ks[5], (D_OUT, D_IN), jnp.float32) * sc, 'bv': jax.random.normal(ks[6], (D_OUT,), jnp.float32) * sc}
    _L0_attn_all = _L0_attn_setup()
    _L0_attn_in = {k: v for k, v in _L0_attn_all.items() if k in ('Wq', 'bq', 'Wk', 'bk', 'Wv', 'bv')}
    del _L0_attn_all

    def _L0_xattn_setup():
        import jax, jax.numpy as jnp
        import numpy as np
        B, L, P = (4, 1024, 256)
        D_MODEL = 256
        D_GLOBAL = 512
        HEADDIM = 32
        EPSILON = 0.001
        RMS_EPS = 1e-05

        def rmsnorm(x, g, eps=RMS_EPS):
            var = jnp.mean(jnp.square(x), axis=-1, keepdims=True)
            return x * jax.lax.rsqrt(var + eps) * g

        def _hnet_depool(h, h_patch_full, patch_lens):
            h_patch = h_patch_full[..., :D_MODEL]
            bsz, plen = (h_patch.shape[0], h_patch.shape[1])
            seqlen = h.shape[1]
            logp = jnp.full((bsz, plen), -EPSILON, dtype=jnp.float32)
            bidx = jnp.cumsum(patch_lens, axis=1) - 1
            boundary_mask = jnp.zeros((bsz, seqlen), dtype=jnp.int32)
            boundary_mask = boundary_mask.at[jnp.arange(bsz)[:, None], bidx].set(1)
            dt = (-jnp.log(-jnp.expm1(logp))).astype(h_patch.dtype)
            x = h_patch / dt[..., None]
            n_heads = D_MODEL // HEADDIM
            A = -jnp.ones((n_heads,), dtype=jnp.float32)
            bcoef = jnp.exp(logp).astype(h_patch.dtype)
            x4 = x.reshape(bsz, plen, n_heads, HEADDIM)
            a = jnp.exp(dt[:, :, None] * A[None, None, :])
            u = (dt * bcoef)[:, :, None, None] * x4
            a_b = jnp.broadcast_to(a[..., None], u.shape)

            def comb(lft, rgt):
                aL, uL = lft
                aR, uR = rgt
                return (aL * aR, uL * aR + uR)
            _, s = jax.lax.associative_scan(comb, (a_b, u), axis=1)
            depool = s.reshape(bsz, plen, D_MODEL)
            plug = jnp.clip(jnp.cumsum(boundary_mask, axis=1) - 1, 0, plen - 1)
            depool_out = depool[jnp.arange(bsz)[:, None], plug]
            return depool_out + h
        key = jax.random.key(seed)
        k1, k2, k3, k4 = jax.random.split(key, 4)
        embeds = jax.random.normal(k1, (B, L, D_MODEL), dtype=jnp.float32)
        patch_embeds = jax.random.normal(k2, (B, P, D_GLOBAL), dtype=jnp.float32)
        patch_lens = jnp.full((B, P), L // P, dtype=jnp.int64)
        W_in = jax.random.normal(k3, (D_MODEL, D_MODEL), dtype=jnp.float32) * 0.02
        b_in = jnp.zeros((D_MODEL,), dtype=jnp.float32)
        g_res = jnp.ones((D_MODEL,), dtype=jnp.float32)
        g_init = jnp.ones((D_GLOBAL,), dtype=jnp.float32)
        return {'embeds': embeds, 'patch_embeds': patch_embeds, 'patch_lens': patch_lens, 'W_in': W_in, 'b_in': b_in, 'g_res': g_res, 'g_init': g_init}
    _L0_xattn_all = _L0_xattn_setup()
    _L0_xattn_in = {k: v for k, v in _L0_xattn_all.items() if k in ('W_in', 'b_in', 'g_res', 'g_init')}
    del _L0_xattn_all

    def _L0_ffn_setup():
        import jax, jax.numpy as jnp
        import numpy as np
        FEATURES = 256
        D_IN = 256

        def fp8_gemm_optimized(x, input_scale, kernel, kernel_scale):
            s_in = input_scale[0]
            s_k = kernel_scale[0]
            x_q = (x.astype(jnp.float32) / s_in).astype(jnp.float8_e4m3fn)
            k_q = (kernel.astype(jnp.float32) / s_k).astype(jnp.float8_e4m3fn)
            y = jnp.dot(x_q.astype(jnp.float32), k_q.astype(jnp.float32), preferred_element_type=jnp.float32)
            return y * (s_in * s_k)
        key = jax.random.key(seed)
        kx, kk, kb = jax.random.split(key, 3)
        x = jax.random.normal(kx, (4, 2048, D_IN), dtype=jnp.float32)
        limit = np.sqrt(6.0 / (D_IN + FEATURES)).astype(np.float32)
        kernel = jax.random.uniform(kk, (D_IN, FEATURES), dtype=jnp.float32, minval=-limit, maxval=limit).astype(jnp.bfloat16)
        input_scale = jnp.ones((1,), dtype=jnp.float32)
        kernel_scale = jnp.ones((1,), dtype=jnp.float32)
        bias = jnp.zeros((FEATURES,), dtype=jnp.bfloat16)
        return {'x': x, 'kernel': kernel, 'input_scale': input_scale, 'kernel_scale': kernel_scale, 'bias': bias}
    _L0_ffn_all = _L0_ffn_setup()
    _L0_ffn_in = {k: v for k, v in _L0_ffn_all.items() if k in ('kernel', 'input_scale', 'kernel_scale', 'bias')}
    del _L0_ffn_all
    return {'x': x, 'ctx_2048': ctx_2048, 'mask_BxS2_if0': mask_BxS2_if0, 'L0_attn_Wq': _L0_attn_in['Wq'], 'L0_attn_bq': _L0_attn_in['bq'], 'L0_attn_Wk': _L0_attn_in['Wk'], 'L0_attn_bk': _L0_attn_in['bk'], 'L0_attn_Wv': _L0_attn_in['Wv'], 'L0_attn_bv': _L0_attn_in['bv'], 'L0_xattn_W_in': _L0_xattn_in['W_in'], 'L0_xattn_b_in': _L0_xattn_in['b_in'], 'L0_xattn_g_res': _L0_xattn_in['g_res'], 'L0_xattn_g_init': _L0_xattn_in['g_init'], 'L0_ffn_kernel': _L0_ffn_in['kernel'], 'L0_ffn_input_scale': _L0_ffn_in['input_scale'], 'L0_ffn_kernel_scale': _L0_ffn_in['kernel_scale'], 'L0_ffn_bias': _L0_ffn_in['bias']}

def reference(x, ctx_2048, mask_BxS2_if0, L0_attn_Wq, L0_attn_bq, L0_attn_Wk, L0_attn_bk, L0_attn_Wv, L0_attn_bv, L0_xattn_W_in, L0_xattn_b_in, L0_xattn_g_res, L0_xattn_g_init, L0_ffn_kernel, L0_ffn_input_scale, L0_ffn_kernel_scale, L0_ffn_bias):
    import jax
    import jax.numpy as jnp

    def _L0_attn_ref(x, Wq, bq, Wk, bk, Wv, bv):
        import jax, jax.numpy as jnp
        import numpy as np
        import math
        B, S, D_IN, D_KQ, D_OUT = (4, 512, 256, 256, 256)
        Q = jnp.einsum('bsd,kd->bsk', x, Wq) + bq
        K = jnp.einsum('bsd,kd->bsk', x, Wk) + bk
        V = jnp.einsum('bsd,od->bso', x, Wv) + bv
        scale = 1.0 / math.sqrt(D_KQ)
        attn = jnp.einsum('bqk,bsk->bqs', Q, K) * scale
        s = attn.shape[-1]
        causal = jnp.tril(jnp.ones((s, s), dtype=bool))
        attn = jnp.where(causal[None, :, :], attn, -jnp.inf)
        attn = jax.nn.softmax(attn, axis=-1)
        Z = jnp.einsum('bqs,bso->bqo', attn, V)
        return Z

    def _L0_xattn_ref(embeds, patch_embeds, patch_lens, W_in, b_in, g_res, g_init):
        import jax, jax.numpy as jnp
        import numpy as np
        B, L, P = (4, 1024, 256)
        D_MODEL = 256
        D_GLOBAL = 512
        HEADDIM = 32
        EPSILON = 0.001
        RMS_EPS = 1e-05

        def rmsnorm(x, g, eps=RMS_EPS):
            var = jnp.mean(jnp.square(x), axis=-1, keepdims=True)
            return x * jax.lax.rsqrt(var + eps) * g

        def _hnet_depool(h, h_patch_full, patch_lens):
            h_patch = h_patch_full[..., :D_MODEL]
            bsz, plen = (h_patch.shape[0], h_patch.shape[1])
            seqlen = h.shape[1]
            logp = jnp.full((bsz, plen), -EPSILON, dtype=jnp.float32)
            bidx = jnp.cumsum(patch_lens, axis=1) - 1
            boundary_mask = jnp.zeros((bsz, seqlen), dtype=jnp.int32)
            boundary_mask = boundary_mask.at[jnp.arange(bsz)[:, None], bidx].set(1)
            dt = (-jnp.log(-jnp.expm1(logp))).astype(h_patch.dtype)
            x = h_patch / dt[..., None]
            n_heads = D_MODEL // HEADDIM
            A = -jnp.ones((n_heads,), dtype=jnp.float32)
            bcoef = jnp.exp(logp).astype(h_patch.dtype)
            x4 = x.reshape(bsz, plen, n_heads, HEADDIM)
            a = jnp.exp(dt[:, :, None] * A[None, None, :])
            u = (dt * bcoef)[:, :, None, None] * x4
            a_b = jnp.broadcast_to(a[..., None], u.shape)

            def comb(lft, rgt):
                aL, uL = lft
                aR, uR = rgt
                return (aL * aR, uL * aR + uR)
            _, s = jax.lax.associative_scan(comb, (a_b, u), axis=1)
            depool = s.reshape(bsz, plen, D_MODEL)
            plug = jnp.clip(jnp.cumsum(boundary_mask, axis=1) - 1, 0, plen - 1)
            depool_out = depool[jnp.arange(bsz)[:, None], plug]
            return depool_out + h
        h = rmsnorm(embeds, g_res)
        h = jnp.einsum('bld,ed->ble', h, W_in) + b_in
        h_patch = rmsnorm(patch_embeds, g_init)
        return _hnet_depool(h, h_patch, patch_lens)

    def _L0_ffn_ref(x, kernel, input_scale, kernel_scale, bias):
        import jax, jax.numpy as jnp
        import numpy as np
        FEATURES = 256
        D_IN = 256

        def fp8_gemm_optimized(x, input_scale, kernel, kernel_scale):
            s_in = input_scale[0]
            s_k = kernel_scale[0]
            x_q = (x.astype(jnp.float32) / s_in).astype(jnp.float8_e4m3fn)
            k_q = (kernel.astype(jnp.float32) / s_k).astype(jnp.float8_e4m3fn)
            y = jnp.dot(x_q.astype(jnp.float32), k_q.astype(jnp.float32), preferred_element_type=jnp.float32)
            return y * (s_in * s_k)
        dtype = jnp.bfloat16
        x = x.astype(dtype)
        orig_shape = x.shape
        x2 = x.reshape(-1, x.shape[-1])
        y = fp8_gemm_optimized(x2, input_scale, kernel, kernel_scale)
        y = y.astype(dtype) + bias
        return y.reshape(orig_shape[:-1] + (FEATURES,))
    x = x + _L0_attn_ref(_layernorm(x, axis=-1), L0_attn_Wq, L0_attn_bq, L0_attn_Wk, L0_attn_bk, L0_attn_Wv, L0_attn_bv)
    x = x + _L0_xattn_ref(_layernorm(x, axis=-1), ctx_2048, mask_BxS2_if0, L0_xattn_W_in, L0_xattn_b_in, L0_xattn_g_res, L0_xattn_g_init)
    x = x + _L0_ffn_ref(_layernorm(x, axis=-1), L0_ffn_kernel, L0_ffn_input_scale, L0_ffn_kernel_scale, L0_ffn_bias)
    return x

_drawn_inputs = setup_inputs


def setup_inputs(seed=0):
    import zlib

    import numpy as np

    out = dict(_drawn_inputs(seed))
    spreads = {'L0_xattn_b_in': (0.0, 0.1),
     'L0_xattn_g_res': (1.0, 0.2),
     'L0_xattn_g_init': (1.0, 0.2),
     'L0_ffn_bias': (0.0, 0.1)}
    factors = {'L0_attn_Wq': 8.0,
     'L0_attn_bq': 8.0,
     'L0_attn_Wk': 8.0,
     'L0_attn_bk': 8.0,
     'L0_attn_Wv': 3.264,
     'L0_attn_bv': 3.011}
    for name, (base, spread) in spreads.items():
        noise = np.random.default_rng([zlib.crc32(name.encode()), seed]).standard_normal(out[name].shape)
        drawn = base * np.exp(spread * noise) if base else spread * noise
        out[name] = jnp.asarray(drawn.astype(out[name].dtype))
    for name, factor in factors.items():
        out[name] = (out[name] * factor).astype(out[name].dtype)
    return out
```

```python
from contextlib import ExitStack
import math

import concourse.bass as bass
from concourse import mybir

F32 = mybir.dt.float32
F32R = mybir.dt.float32r
BF16 = mybir.dt.bfloat16
I32 = mybir.dt.int32
ALU = mybir.AluOpType
ACT = mybir.ActivationFunctionType
AX = mybir.AxisListType

P = 128
LN_EPS = 1e-5
RMS_EPS = 1e-5
PATCH_EPS = 0.001
PATCH_B = math.exp(-PATCH_EPS)
PATCH_A = -math.expm1(-PATCH_EPS)
E4M3_MAX = 464.0
MASKED = -3.0e38
GROUP = 4
S_BANKS = 3
T_BANKS = 2
PT_SLOTS = 3


def chunks_of(i):
    return i // GROUP + 1


def blocks_of(i, j):
    return min(GROUP, i + 1 - GROUP * j)


def make_plan(tiles):
    groups = tiles // GROUP
    plan = [("turn_w", 0, 0), ("xnorm", 0, 0), ("turn_w", 1, 0), ("turn_w", 2, 0),
            ("turn_x", 0, 0), ("turn_x", 0, 1)]
    front = {0: [("xnorm", 1, 0), ("turn_w", 3, 0), ("quant_k", 0, 0)],
             1: [("xnorm", 2, 0), ("ends_sum", 0, 0)],
             2: [("xnorm", 3, 0), ("ends_place", 0, 0)]}
    for g in range(groups - 1):
        for m in range(6):
            plan.append(("proj", g, m))
            if m == 1:
                plan.append(front[g][0])
            if m == 3:
                plan += front[g][1:]
        plan += [("turn_x", g + 1, 0), ("turn_x", g + 1, 1)]
        if g == 1:
            plan.append(("patch_norm", 0, 0))
    late = [[("proj", groups - 1, 0), ("proj", groups - 1, 1), ("ends_count", 0, 0)],
            [("proj", groups - 1, 2), ("proj", groups - 1, 3), ("patch_scan", 0, 0)],
            [("proj", groups - 1, 4), ("patch_fix", 0, 0)],
            [("proj", groups - 1, 5), ("gather", 0, 0)]]
    first = 6
    start_b = []
    for b in range(tiles):
        start_b.append(max(b + 2, first + b // 2))
    for t in range(tiles + 3):
        out_now = [t - 2] if 0 <= t - 2 < tiles else []
        b_now = [b for b in range(tiles) if start_b[b] == t]
        c_now = [b for b in range(tiles) if start_b[b] + 1 == t]
        n = chunks_of(t) if t < tiles else 0
        scores = [("score", t, j) for j in range(n)]
        plan += scores[:1]
        plan += [("attn_out", b, 0) for b in out_now]
        plan += scores[1:2]
        plan += [("y", b, 0) for b in b_now]
        plan += scores[2:]
        if t < tiles:
            plan.append(("soft", t, 0))
        if t < len(late):
            plan += late[t]
        plan += [("turn_y", b, 0) for b in b_now[:1]]
        plan += [("turn_q", b, 0) for b in c_now[:1]]
        s = t - 1
        n = chunks_of(s) if 0 <= s < tiles else 0
        inner = [[("h", b, 0) for b in b_now[:1]] + [("turn_y", b, 0) for b in b_now[1:]]
                 + [("ffn", b, 0) for b in c_now[:1]] + [("turn_q", b, 0) for b in c_now[1:]],
                 [("z", b, 0) for b in b_now[:1]] + [("h", b, 0) for b in b_now[1:]]
                 + [("ffn", b, 0) for b in c_now[1:]],
                 [("z", b, 0) for b in b_now[1:]]]
        for j in range(max(n + 1, len(inner))):
            if j < n:
                plan.append(("turn_p", s, j))
            if j < len(inner):
                plan += inner[j]
            if 1 <= j <= n:
                plan.append(("pv", s, j - 1))
    return plan


def decoder_layer(nc, x, ctx_in, lens, Wq, bq, Wk, bk, Wv, bv, W_in, b_in, g_res, g_init,
                  ffn_w, s_in, s_k, ffn_b, table, out):
    _, S, D = x.shape
    _, NPATCH, DG = ctx_in.shape
    TILES = S // P
    DC = D // P
    PER = -(-NPATCH // P)
    FULL = NPATCH // PER
    REST = NPATCH - FULL * PER
    PP = FULL + 1
    SCALE = 1.0 / math.sqrt(D)
    assert D == 256 and S % (P * GROUP) == 0 and 0 < REST < PER and DG == 2 * D
    PLAN = make_plan(TILES)

    s_use = {st: n for n, st in enumerate(st for st in PLAN if st[0] in ("proj", "score"))}
    t_use = {st: n for n, st in enumerate(st for st in PLAN if st[0] in ("turn_w", "turn_x", "turn_p"))}
    p_use = {st[1:]: n for n, st in enumerate(st for st in PLAN if st[0] == "turn_p")}
    norm_no = {st: n for n, st in enumerate(st for st in PLAN if st[0] in ("xnorm", "attn_out", "h"))}
    high_no = {st: n for n, st in enumerate(st for st in PLAN if st[0] == "proj")}
    assert [st[1] for st in PLAN if st[0] == "h"] == list(range(TILES))

    x_t = x.rearrange("a (t p) d -> p (a t) d", p=P)
    out_t = out.rearrange("a (t p) d -> p (a t) d", p=P)
    ctx_rows = ctx_in.rearrange("a r d -> (a r) d")

    ctx = ExitStack()
    with ctx:
        def sb(name, shape, dt=F32):
            return ctx.enter_context(nc.sbuf_tensor(name, shape, dt))

        def bank(name):
            return ctx.enter_context(nc.psum_tensor(name, [P, 512], F32))

        def sem(name):
            return ctx.enter_context(nc.semaphore(name))

        X = sb("X", [P, TILES, D])
        XN = sb("XN", [P, GROUP, D])
        XT_h = sb("XT_h", [P, 2, DC, GROUP * P], F32R)
        XT_l = sb("XT_l", [P, 2, DC, GROUP * P], F32R)
        QT_h = sb("QT_h", [P, DC, S - GROUP * P], F32R)
        QT_l = sb("QT_l", [P, DC, S - GROUP * P], F32R)
        KT_h = sb("KT_h", [P, DC, S], F32R)
        KT_l = sb("KT_l", [P, DC, S], F32R)
        V = sb("V", [P, TILES, 2, D], F32R)
        SC = sb("SC", [P, 2, S])
        PT_h = sb("PT_h", [P, PT_SLOTS, GROUP * P], F32R)
        PT_l = sb("PT_l", [P, PT_SLOTS, GROUP * P], F32R)
        Wraw = [SC[:, 0, 512 * m:512 * m + 512].rearrange("p (b d) -> p b d", b=2) for m in range(4)]
        WT_h = sb("WT_h", [P, 4, DC, D], F32R)
        WT_l = sb("WT_l", [P, 4, DC, D], F32R)
        CT = sb("CT", [P, PER, DG])
        GB = CT[:, 0:TILES // 2, :].rearrange("p k (h d) -> p (k h) d", h=2)
        late = CT[:, TILES // 2:PER, :].rearrange("p k d -> p (k d)")
        Y, VV, MG = (late[:, 512 * n:512 * (n + 1)].rearrange("p (s d) -> p s d", s=2) for n in range(3))
        Z, Q8, F1 = (late[:, 1536 + 256 * n:1792 + 256 * n].bitcast(BF16).rearrange("p (s d) -> p s d", s=2)
                     for n in range(3))
        Olow = XN[:, 0:2, :]
        carry = XN[:, 2, :]
        bv_b = sb("bv_b", [P, D])
        bin_b = sb("bin_b", [P, D])
        ginit_b = sb("ginit_b", [P, D])
        fb_b = sb("fb_b", [P, D], BF16)
        cols = sb("cols", [P, 3, DC])
        scl = sb("scl", [P, 4])
        ss = sb("ss", [P, 1])
        identf = sb("identf", [P, P])
        identb = sb("identb", [P, P], BF16)
        maskb = sb("maskb", [P, P], BF16)
        tri = SC[:, 1, S - P:S]
        trib = sb("trib", [P, P], BF16)
        onesb = sb("onesb", [P, P], BF16)
        seam = sb("seam", [P, P])
        neg_half = sb("neg_half", [P, 16])
        stats = sb("stats", [P, 3, GROUP, 6])
        mv = sb("mv", [P, 3 * TILES, 2])
        rs = sb("rs", [P, 3 * TILES])
        ve = sb("ve", [P, 3 * TILES])
        cmin = sb("cmin", [P, 2, GROUP])
        nmax = sb("nmax", [P, 2])
        lsum = sb("lsum", [P, 2])
        rl = sb("rl", [P, 2])
        YT_h = sb("YT_h", [P, DC, P], F32R)
        YT_l = sb("YT_l", [P, DC, P], F32R)
        zmax = sb("zmax", [P, 2])
        nanf = sb("nanf", [P, 2, 2])
        QT8 = sb("QT8", [P, DC, P], BF16)
        kraw = sb("kraw", [P, DC, D], BF16)
        kv, km = (SC[:, 1, 512 * n:512 * (n + 1)].rearrange("p (c e) -> p c e", c=DC) for n in range(2))
        kq = sb("kq", [P, DC, D], BF16)
        ln = sb("ln", [P, PER], I32)
        limb = sb("limb", [P, 3, PER], I32)
        limf = sb("limf", [P, 3, PER])
        limc = sb("limc", [P, 3, PER])
        limp = sb("limp", [P, 3])
        limt = sb("limt", [P, 3, PER], I32)
        endi = sb("endi", [P, 4, PER], I32)
        endf = sb("endf", [P, 4, PER])
        iota = sb("iota", [P, P], BF16)
        hot_lo = SC[:, 1, S // 2:S // 2 + PER * P // 2].bitcast(BF16).rearrange("p (k r) -> p k r", r=P)
        hot_hi = sb("hot_hi", [P, PER, TILES], BF16)
        onef = sb("onef", [P, 16])
        bmask = sb("bmask", [P, TILES], BF16)
        btot = sb("btot", [P, 4, TILES])
        plug = sb("plug", [P, TILES], I32)
        ssq = sb("ssq", [P, PER])
        prs = sb("prs", [P, PER])

        S_B = [bank(f"S_B{n}") for n in range(S_BANKS)]
        T_B = [bank(f"T_B{n}") for n in range(T_BANKS)]
        O_B = bank("O_B")
        Y_B = bank("Y_B")
        Q_B = bank("Q_B")

        x_in = [sem(f"x_in{g}") for g in range(TILES // GROUP)]
        w_in = [sem(f"w_in{m}") for m in range(4)]
        cols_in = sem("cols_in")
        rows_in = sem("rows_in")
        kern_in = sem("kern_in")
        lens_in = sem("lens_in")
        ctx_loaded = sem("ctx_loaded")
        const_ready = sem("const_ready")
        const_step = sem("const_step")
        scl_ready = sem("scl_ready")
        stats_ready = sem("stats_ready")
        mv_ready = sem("mv_ready")
        ve_ready = sem("ve_ready")
        rs_ready = sem("rs_ready")
        xn_ready = sem("xn_ready")
        xb_ready = sem("xb_ready")
        s_filled = sem("s_filled")
        s_high = sem("s_high")
        s_freed = sem("s_freed")
        t_filled = sem("t_filled")
        t_high = sem("t_high")
        t_freed = sem("t_freed")
        min_ready = sem("min_ready")
        probs_ready = sem("probs_ready")
        rl_ready = sem("rl_ready")
        pv_done = sem("pv_done")
        olow_ready = sem("olow_ready")
        olow_added = sem("olow_added")
        x1_ready = sem("x1_ready")
        y_ready = sem("y_ready")
        patches_added = sem("patches_added")
        yt_filled = sem("yt_filled")
        yt_high = sem("yt_high")
        yt_low = sem("yt_low")
        h_done = sem("h_done")
        x2_ready = sem("x2_ready")
        z_ready = sem("z_ready")
        v_ready = sem("v_ready")
        z_ready_max = sem("z_ready_max")
        z_scaled = sem("z_scaled")
        ends_conv = sem("ends_conv")
        bits_ready = sem("bits_ready")
        magic_ready = sem("magic_ready")
        nan_step = sem("nan_step")
        round_step = sem("round_step")
        q_ready = sem("q_ready")
        qt_filled = sem("qt_filled")
        qt_ready = sem("qt_ready")
        ffn_done = sem("ffn_done")
        f_ready = sem("f_ready")
        f_step = sem("f_step")
        out_ready = sem("out_ready")
        out_stored = sem("out_stored")
        kq_step = sem("kq_step")
        kq_pool = sem("kq_pool")
        kq_ready = sem("kq_ready")
        ends_dve = sem("ends_dve")
        ends_pool = sem("ends_pool")
        ends_pe = sem("ends_pe")
        patch_sq = sem("patch_sq")
        patch_rs = sem("patch_rs")
        patch_u = sem("patch_u")
        patch_dve = sem("patch_dve")
        patch_pe = sem("patch_pe")
        carry_ready = sem("carry_ready")
        table_stored = sem("table_stored")
        gathered = sem("gathered")
        gb_step = sem("gb_step")
        gb_ready = sem("gb_ready")

        def q_part(part, g):
            if g == TILES // GROUP - 1:
                return (XT_h, XT_l)[part][:, (g - 1) % 2, :, :]
            return (QT_h, QT_l)[part][:, :, g * GROUP * P:(g + 1) * GROUP * P]

        def k_part(part, g):
            return (KT_h, KT_l)[part][:, :, g * GROUP * P:(g + 1) * GROUP * P]

        block = ctx.enter_context(nc.Block())

        def norm_cols(st):
            kind, a, _ = st
            first = {"xnorm": GROUP * a, "attn_out": TILES + a, "h": 2 * TILES + a}[kind]
            return slice(first, first + norm_tiles(st))

        def norm_tiles(st):
            return GROUP if st[0] == "xnorm" else 1

        norm_cum = {}
        total = 0
        for st in sorted(norm_no, key=lambda q: norm_no[q]):
            total += norm_tiles(st)
            norm_cum[st] = total
        xn_cum = {g: GROUP * (g + 1) for g in range(TILES // GROUP)}

        @block.sync
        def _(sp):
            sp.dma_start(X[:, 0:GROUP, :], x_t[:, 0:GROUP, :]).then_inc(x_in[0], 16)
            for m, w in enumerate((Wq, Wk, Wv)):
                sp.dma_start(Wraw[m], w.rearrange("(b p) d -> p b d", p=P)).then_inc(w_in[m], 16)
            sp.dma_start(X[:, GROUP:2 * GROUP, :], x_t[:, GROUP:2 * GROUP, :]).then_inc(x_in[1], 16)
            sp.dma_start(Wraw[3], W_in.rearrange("(b p) d -> p b d", p=P)).then_inc(w_in[3], 16)
            sp.dma_start(CT[0:FULL, :, :],
                         ctx_rows[0:FULL * PER, :].rearrange("(p k) d -> p k d", k=PER)).then_inc(ctx_loaded, 16)
            sp.dma_start(CT[FULL:PP, 0:REST, :],
                         ctx_rows[FULL * PER:NPATCH, :].rearrange("(p k) d -> p k d", k=REST)).then_inc(ctx_loaded, 16)
            sp.dma_start(CT[FULL:PP, REST:PER, :],
                         ctx_rows[0:PER - REST, :].rearrange("(p k) d -> p k d", k=PER - REST)).then_inc(ctx_loaded, 16)
            for g in range(2, TILES // GROUP):
                sp.dma_start(X[:, g * GROUP:(g + 1) * GROUP, :],
                             x_t[:, g * GROUP:(g + 1) * GROUP, :]).then_inc(x_in[g], 16)
            sp.dma_start(kraw[:, :, :], ffn_w.rearrange("(c p) e -> p c e", p=P)).then_inc(kern_in, 16)
            sp.wait_ge(patch_dve, 2 * PER)
            sp.dma_start(table[0:FULL * PER, :].rearrange("(p k) d -> p k d", k=PER),
                         CT[0:FULL, :, 0:D]).then_inc(table_stored, 16)
            sp.dma_start(table[FULL * PER:NPATCH, :].rearrange("(p k) d -> p k d", k=REST),
                         CT[FULL:PP, 0:REST, 0:D]).then_inc(table_stored, 16)
            for b in range(TILES):
                sp.wait_ge(out_ready, b + 1)
                sp.dma_start(out_t[:, b, :], X[:, b, :]).then_inc(out_stored, 16)
            sp.wait_ge(out_stored, 16 * TILES)
            sp.wait_ge(table_stored, 32)

        @block.gpsimd
        def _(pool):
            pool.memset(identf[:, :], 0.0).then_inc(const_step, 1)
            pool.memset(identb[:, :], 0.0).then_inc(const_step, 1)
            pool.memset(maskb[:, :], 0.0).then_inc(const_step, 1)
            pool.memset(tri[:, :], 0.0).then_inc(const_step, 1)
            pool.memset(trib[:, :], 1.0).then_inc(const_step, 1)
            pool.memset(seam[:, :], 0.0).then_inc(const_step, 1)
            pool.memset(onesb[:, :], 1.0).then_inc(const_ready, 1)
            pool.memset(neg_half[:, :], -0.5).then_inc(const_ready, 1)
            pool.memset(onef[:, :], 1.0).then_inc(const_ready, 1)
            pool.wait_ge(const_step, 6)
            for m in (identf, identb):
                pool.affine_select(out=m[:, :], in_=m[:, :], compare_op=ALU.not_equal, fill=1.0, base=0,
                                   pattern=[[-1, P]], channel_multiplier=1).then_inc(const_ready, 1)
            pool.affine_select(out=maskb[:, :], in_=maskb[:, :], compare_op=ALU.is_ge, fill=MASKED, base=0,
                               pattern=[[-1, P]], channel_multiplier=1).then_inc(const_ready, 1)
            pool.wait_ge(const_ready, 5)
            pool.memset(ln[:, :], 0).then_inc(const_step, 1)
            pool.affine_select(out=tri[:, :], in_=tri[:, :], compare_op=ALU.is_ge, fill=1.0, base=0,
                               pattern=[[-1, P]], channel_multiplier=1).then_inc(const_ready, 1)
            pool.affine_select(out=trib[:, :], in_=trib[:, :], compare_op=ALU.is_ge, fill=0.0, base=0,
                               pattern=[[1, P]], channel_multiplier=-1).then_inc(const_ready, 1)
            pool.affine_select(out=seam[:, :], in_=seam[:, :], compare_op=ALU.not_equal, fill=1.0, base=1,
                               pattern=[[-1, P]], channel_multiplier=1).then_inc(const_step, 1)
            pool.wait_ge(const_step, 8)
            pool.affine_select(out=seam[:, :], in_=seam[:, :], compare_op=ALU.not_equal,
                               fill=PATCH_A ** PER, base=2,
                               pattern=[[-1, P]], channel_multiplier=1).then_inc(const_ready, 1)
            pool.iota(iota[:, :], pattern=[[1, P]], base=0, channel_multiplier=0,
                      allow_small_or_imprecise_dtypes=True).then_inc(const_ready, 1)
            pool.dma_start(ln[0:FULL, :], lens[0, 0:FULL * PER].rearrange("(p k) -> p k", k=PER)).then_inc(lens_in, 16)
            pool.dma_start(ln[FULL:PP, 0:REST],
                           lens[0, FULL * PER:NPATCH].rearrange("(p k) -> p k", k=REST)).then_inc(lens_in, 16)

            def rsqrt_of_var(st, mul, add):
                s, n, no = norm_cols(st), norm_tiles(st), norm_no[st]
                pool.wait_ge(mv_ready, norm_cum[st])
                pool.tensor_scalar(ve[:, s], mv[:, s, 1], mul, add, ALU.mult, ALU.add).then_inc(ve_ready, 1)
                pool.wait_ge(ve_ready, no + 1)
                pool.tensor_tensor(rs[:, s], ve[:, s], neg_half[:, 0:n], ALU.pow).then_inc(rs_ready, 1)

            for st in PLAN:
                kind, a, b = st
                if kind == "xnorm":
                    rsqrt_of_var(st, 1.0, LN_EPS)
                    pool.wait_ge(rows_in, 64)
                    pool.wait_ge(xn_ready, xn_cum[a])
                    for t in range(GROUP * a, GROUP * a + GROUP):
                        pool.tensor_tensor(X[:, t, :], X[:, t, :], bv_b[:, :], ALU.add).then_inc(xb_ready, 1)
                elif kind == "attn_out":
                    pool.wait_ge(olow_ready, a + 1)
                    pool.wait_ge(xb_ready, a + 1)
                    pool.tensor_tensor(X[:, a, :], X[:, a, :], Olow[:, a % 2, :], ALU.add).then_inc(olow_added, 1)
                    rsqrt_of_var(st, 1.0 + RMS_EPS, RMS_EPS * LN_EPS)
                elif kind == "y":
                    pool.wait_ge(gb_ready, a + 1)
                    pool.wait_ge(y_ready, a + 1)
                    pool.tensor_tensor(X[:, a, :], X[:, a, :], GB[:, a, :], ALU.add).then_inc(patches_added, 1)
                elif kind == "h":
                    rsqrt_of_var(st, 1.0, LN_EPS)
                elif kind == "z":
                    pool.wait_ge(magic_ready, a + 1)
                    pool.tensor_tensor(VV[:, a % 2, :], VV[:, a % 2, :], MG[:, a % 2, :], ALU.add).then_inc(round_step, 1)
                    pool.wait_ge(round_step, a + 1)
                    if a >= 2:
                        pool.wait_ge(qt_filled, a - 1)
                    pool.tensor_tensor(Q8[:, a % 2, :], VV[:, a % 2, :], MG[:, a % 2, :],
                                       ALU.subtract).then_inc(q_ready, 1)
                elif kind == "ffn":
                    pool.wait_ge(f_ready, a + 1)
                    pool.tensor_tensor(F1[:, a % 2, :], F1[:, a % 2, :], fb_b[:, :], ALU.add).then_inc(f_step, 1)
                    pool.wait_ge(f_step, a + 1)
                    pool.tensor_tensor(X[:, a, :], X[:, a, :], F1[:, a % 2, :], ALU.add).then_inc(out_ready, 1)
                elif kind == "quant_k":
                    pool.wait_ge(kq_step, 3)
                    pool.tensor_tensor(kv[:, :, :], kv[:, :, :], km[:, :, :], ALU.add).then_inc(kq_pool, 1)
                    pool.wait_ge(kq_pool, 1)
                    pool.tensor_tensor(kv[:, :, :], kv[:, :, :], km[:, :, :], ALU.subtract).then_inc(kq_pool, 1)
                elif kind == "ends_sum":
                    pool.wait_ge(ends_dve, 11)
                    pool.tensor_tensor(endi[:, 0, :], limt[:, 0, :], limt[:, 1, :], ALU.add).then_inc(ends_pool, 1)
                    pool.wait_ge(ends_pool, 1)
                    pool.tensor_tensor(endi[:, 0, :], endi[:, 0, :], limt[:, 2, :], ALU.add).then_inc(ends_pool, 1)
                elif kind == "patch_norm":
                    pool.wait_ge(patch_sq, PER)
                    pool.tensor_scalar(prs[0:PP, :], ssq[0:PP, :], 1.0 / DG, RMS_EPS, ALU.mult, ALU.add).then_inc(patch_rs, 1)
                    pool.wait_ge(patch_rs, 1)
                    pool.tensor_tensor(prs[0:PP, :], prs[0:PP, :], neg_half[0:PP, 0:PER], ALU.pow).then_inc(patch_rs, 1)
                    pool.wait_ge(patch_rs, 2)
                    pool.tensor_scalar(prs[0:PP, :], prs[0:PP, :], PATCH_B, 0.0, ALU.mult, ALU.add).then_inc(patch_rs, 1)
                elif kind == "gather":
                    pool.wait_ge(table_stored, 32)
                    pool.wait_ge(ends_dve, 27)
                    for t in range(TILES):
                        pool.indirect_dma_start(GB[:, t, :], None, table[:, :],
                                                bass.IndirectOffsetOnAxis(plug[:, t:t + 1].bitcast(mybir.dt.uint32), 0),
                                                bounds_check=NPATCH - 1).then_inc(gathered, 16)
                    for t in range(TILES):
                        pool.wait_ge(gathered, 16 * TILES)
                        pool.tensor_tensor(GB[:, t, :], GB[:, t, :], ginit_b[:, :], ALU.mult).then_inc(gb_step, 1)
                        pool.wait_ge(gb_step, t + 1)
                        pool.tensor_tensor(GB[:, t, :], GB[:, t, :], bin_b[:, :], ALU.add).then_inc(gb_ready, 1)

        @block.scalar
        def _(act):
            act.dma_start(cols[:, 0, :], bq.rearrange("(c p) -> p c", p=P), allow_slow_non_contiguous=True).then_inc(cols_in, 16)
            act.dma_start(cols[:, 1, :], bk.rearrange("(c p) -> p c", p=P), allow_slow_non_contiguous=True).then_inc(cols_in, 16)
            act.dma_start(cols[:, 2, :], g_res.rearrange("(c p) -> p c", p=P), allow_slow_non_contiguous=True).then_inc(cols_in, 16)
            act.dma_start(scl[:, 0:1], s_in.rearrange("(a n) -> a n", a=1).to_broadcast((P, 1))).then_inc(cols_in, 16)
            act.dma_start(scl[:, 1:2], s_k.rearrange("(a n) -> a n", a=1).to_broadcast((P, 1))).then_inc(cols_in, 16)
            for dst, src, n in ((bv_b, bv, D), (bin_b, b_in, D), (ginit_b, g_init[0:D], D), (fb_b, ffn_b, D)):
                act.dma_start(dst[:, :], src.rearrange("(a n) -> a n", a=1).to_broadcast((P, n))).then_inc(rows_in, 16)

            for st in PLAN:
                kind, a, b = st
                if kind == "turn_w":
                    n = t_use[st]
                    act.wait_ge(t_filled, n + 1)
                    src = T_B[n % T_BANKS][:, :].rearrange("p (c e) -> p c e", c=DC)
                    if a == 3:
                        act.wait_ge(cols_in, 80)
                        act.activation(WT_h[:, a, 0, :], src[:, 0, :], ACT.Copy, scale=cols[:, 2, 0:1])
                        act.activation(WT_h[:, a, 1, :], src[:, 1, :], ACT.Copy,
                                       scale=cols[:, 2, 1:2]).then_inc(t_high, 1)
                    else:
                        act.activation(WT_h[:, a, :, :], src, ACT.Copy).then_inc(t_high, 1)
                elif kind == "turn_x":
                    n = t_use[st]
                    act.wait_ge(t_filled, n + 1)
                    if a >= 2:
                        act.wait_ge(s_filled, s_use[("proj", a - 2, 5)] + 1)
                    act.activation(XT_h[:, a % 2, b, :], T_B[n % T_BANKS][:, :], ACT.Copy).then_inc(t_high, 1)
                elif kind == "turn_p":
                    n, k, w = t_use[st], p_use[(a, b)], P * blocks_of(a, b)
                    act.wait_ge(t_filled, n + 1)
                    if k >= PT_SLOTS:
                        act.wait_ge(pv_done, k - PT_SLOTS + 1)
                    act.activation(PT_h[:, k % PT_SLOTS, 0:w], T_B[n % T_BANKS][:, 0:w], ACT.Copy).then_inc(t_high, 1)
                elif kind == "proj":
                    n = s_use[st]
                    act.wait_ge(s_filled, n + 1)
                    src = S_B[n % S_BANKS][:, :]
                    if b < 4:
                        act.wait_ge(cols_in, 80)
                        dst = (q_part, k_part)[b // 2](0, a)[:, b % 2, :]
                        act.activation(dst, src, ACT.Identity, bias=cols[:, b // 2, b % 2:b % 2 + 1]).then_inc(s_high, 1)
                    else:
                        t = GROUP * a + 2 * (b - 4)
                        act.activation(V[:, t:t + 2, 0, :], src.rearrange("p (t d) -> p t d", t=2),
                                       ACT.Copy).then_inc(s_high, 1)
                elif kind == "soft":
                    w = P * (a + 1)
                    act.wait_ge(min_ready, a + 1)
                    if a >= 2:
                        act.wait_ge(rl_ready, a - 1)
                    act.activation(SC[:, a % 2, 0:w], SC[:, a % 2, 0:w], ACT.Exp, scale=-1.0,
                                   bias=nmax[:, a % 2:a % 2 + 1],
                                   accum_out=lsum[:, a % 2:a % 2 + 1]).then_inc(probs_ready, 1)
                elif kind == "attn_out":
                    act.wait_ge(pv_done, p_use[(a, chunks_of(a) - 1)] + 1)
                    act.wait_ge(rl_ready, a + 1)
                    if a >= 2:
                        act.wait_ge(olow_added, a - 1)
                    act.activation(Olow[:, a % 2, :], O_B[:, D:2 * D], ACT.Copy,
                                   scale=rl[:, a % 2:a % 2 + 1]).then_inc(olow_ready, 1)
                elif kind == "turn_y":
                    act.wait_ge(yt_filled, a + 1)
                    act.activation(YT_h[:, :, :], Y_B[:, 0:D].rearrange("p (c r) -> p c r", c=DC),
                                   ACT.Copy).then_inc(yt_high, 1)
                elif kind == "turn_q":
                    act.wait_ge(qt_filled, a + 1)
                    act.activation(QT8[:, :, :], Q_B[:, 0:P].bitcast(BF16).rearrange("p (c r) -> p c r", c=DC),
                                   ACT.Copy).then_inc(qt_ready, 1)
                elif kind == "ffn":
                    act.wait_ge(ffn_done, a + 1)
                    act.wait_ge(nan_step, 2 * (a + 1))
                    if a >= 2:
                        act.wait_ge(out_ready, a - 1)
                    act.activation(F1[:, a % 2, :], Q_B[:, 0:D], ACT.Identity, scale=ss[:, 0:1],
                                   bias=nanf[:, a % 2, 1:2]).then_inc(f_ready, 1)
                elif kind == "patch_norm":
                    act.wait_ge(ctx_loaded, 48)
                    for k in range(PER):
                        if k >= 2:
                            act.wait_ge(patch_sq, k - 1)
                        act.activation((O_B, Y_B)[k % 2][0:PP, :], CT[0:PP, k, :], ACT.Square,
                                       accum_out=ssq[0:PP, k:k + 1]).then_inc(patch_sq, 1)
                elif kind == "patch_scan":
                    act.wait_ge(patch_rs, 3)
                    for k in range(PER):
                        act.activation(CT[0:PP, k, 0:D], CT[0:PP, k, 0:D], ACT.Copy,
                                       scale=prs[0:PP, k:k + 1]).then_inc(patch_u, 1)
                elif kind == "patch_fix":
                    act.wait_ge(patch_pe, 1)
                    act.activation(carry[0:PP, :], Y_B[0:PP, 0:D], ACT.Copy).then_inc(carry_ready, 1)

        @block.tensor
        def _(pe):
            pe.wait_ge(const_ready, 6)

            def three_pass(ps, st_h, st_l, mv_h, mv_l, first, last):
                pe.matmul(ps, st_h, mv_h, start=first, stop=False)
                pe.matmul(ps, st_h, mv_l, start=False, stop=False)
                return pe.matmul(ps, st_l, mv_h, start=False, stop=last)

            def take_s(st):
                n = s_use[st]
                if n >= S_BANKS:
                    pe.wait_ge(s_freed, n - S_BANKS + 1)
                return S_B[n % S_BANKS]

            def take_t(st):
                n = t_use[st]
                if n >= T_BANKS:
                    pe.wait_ge(t_freed, n - T_BANKS + 1)
                return T_B[n % T_BANKS]

            for st in PLAN:
                kind, a, b = st
                if kind == "turn_w":
                    pe.wait_ge(w_in[a], 16)
                    ps = take_t(st)
                    for c in range(DC):
                        for e in range(DC):
                            mm = pe.transpose(ps[:, c * D + e * P:c * D + (e + 1) * P],
                                              Wraw[a][:, e, c * P:(c + 1) * P], identf[:, :])
                    mm.then_inc(t_filled, 1)
                elif kind == "turn_x":
                    pe.wait_ge(xn_ready, xn_cum[a])
                    ps = take_t(st)
                    for t in range(GROUP):
                        mm = pe.transpose(ps[:, t * P:(t + 1) * P], XN[:, t, b * P:(b + 1) * P], identf[:, :])
                    mm.then_inc(t_filled, 1)
                elif kind == "proj":
                    pe.wait_ge(t_freed, t_use[("turn_x", a, 1)] + 1)
                    pe.wait_ge(t_freed, t_use[("turn_w", b // 2, 0)] + 1)
                    ps, g = take_s(st), a % 2
                    if b < 4:
                        w, e = b // 2, slice((b % 2) * P, (b % 2 + 1) * P)
                        for c in range(DC):
                            mm = three_pass(ps[:, :], WT_h[:, w, c, e], WT_l[:, w, c, e],
                                            XT_h[:, g, c, :], XT_l[:, g, c, :], c == 0, c == DC - 1)
                    else:
                        for u in range(2):
                            r = slice((2 * (b - 4) + u) * P, (2 * (b - 4) + u + 1) * P)
                            for c in range(DC):
                                mm = three_pass(ps[:, u * D:(u + 1) * D], XT_h[:, g, c, r], XT_l[:, g, c, r],
                                                WT_h[:, 2, c, :], WT_l[:, 2, c, :], c == 0, c == DC - 1)
                    mm.then_inc(s_filled, 1)
                elif kind == "score":
                    for g, m in ((a // GROUP, 1), (b, 3)):
                        pe.wait_ge(s_freed, s_use[("proj", g, m)] + 1)
                    ps, n = take_s(st), blocks_of(a, b)
                    g, r = a // GROUP, slice(a % GROUP * P, (a % GROUP + 1) * P)
                    diagonal = b == chunks_of(a) - 1
                    for c in range(DC):
                        mm = three_pass(ps[:, 0:n * P], q_part(0, g)[:, c, r], q_part(1, g)[:, c, r],
                                        k_part(0, b)[:, c, 0:n * P], k_part(1, b)[:, c, 0:n * P],
                                        c == 0, c == DC - 1 and not diagonal)
                    if diagonal:
                        mm = pe.matmul(ps[:, (n - 1) * P:n * P], identb[:, :], maskb[:, :], start=False, stop=True)
                    mm.then_inc(s_filled, 1)
                elif kind == "turn_p":
                    pe.wait_ge(probs_ready, a + 1)
                    ps = take_t(st)
                    for u in range(blocks_of(a, b)):
                        k = (b * GROUP + u) * P
                        mm = pe.transpose(ps[:, u * P:(u + 1) * P], SC[:, a % 2, k:k + P], identf[:, :])
                    mm.then_inc(t_filled, 1)
                elif kind == "pv":
                    pe.wait_ge(t_freed, t_use[("turn_p", a, b)] + 1)
                    if b == 0:
                        if a >= 1:
                            pe.wait_ge(x1_ready, a)
                    slot, n = p_use[(a, b)] % PT_SLOTS, blocks_of(a, b)
                    pe.wait_ge(s_freed, s_use[("proj", b, 5)] + 1 if n > 2 else s_use[("proj", b, 4)] + 1)
                    for u in range(n):
                        t, r = b * GROUP + u, slice(u * P, (u + 1) * P)
                        pe.matmul(O_B[:, :], PT_h[:, slot, r], V[:, t, :, :], start=(t == 0), stop=False)
                        mm = pe.matmul(O_B[:, 0:D], PT_l[:, slot, r], V[:, t, 0, :], start=False, stop=(t == a))
                    mm.then_inc(pv_done, 1)
                elif kind == "turn_y":
                    pe.wait_ge(y_ready, a + 1)
                    if a == 0:
                        pe.wait_ge(carry_ready, 1)
                    if a >= 1:
                        pe.wait_ge(x2_ready, a)
                    for c in range(DC):
                        mm = pe.transpose(Y_B[:, c * P:(c + 1) * P], Y[:, a % 2, c * P:(c + 1) * P], identf[:, :])
                    mm.then_inc(yt_filled, 1)
                elif kind == "h":
                    pe.wait_ge(yt_low, a + 1)
                    pe.wait_ge(t_freed, t_use[("turn_w", 3, 0)] + 1)
                    for c in range(DC):
                        mm = three_pass(Y_B[:, 0:D], YT_h[:, c, :], YT_l[:, c, :], WT_h[:, 3, c, :], WT_l[:, 3, c, :],
                                        c == 0, c == DC - 1)
                    mm.then_inc(h_done, 1)
                elif kind == "turn_q":
                    pe.wait_ge(q_ready, a + 1)
                    if a >= 1:
                        pe.wait_ge(f_ready, a)
                    if a == 0:
                        pe.wait_ge(ends_dve, 23)
                    for c in range(DC):
                        mm = pe.transpose(Q_B[:, 0:P].bitcast(BF16)[:, c * P:(c + 1) * P],
                                          Q8[:, a % 2, c * P:(c + 1) * P], identb[:, :])
                    mm.then_inc(qt_filled, 1)
                elif kind == "ffn":
                    pe.wait_ge(qt_ready, a + 1)
                    pe.wait_ge(kq_ready, 1)
                    for c in range(DC):
                        mm = pe.matmul(Q_B[:, 0:D], QT8[:, c, :], kq[:, c, :], start=(c == 0), stop=(c == DC - 1))
                    mm.then_inc(ffn_done, 1)
                elif kind == "ends_sum":
                    pe.wait_ge(const_ready, 10)
                    pe.wait_ge(ends_dve, 6)
                    pe.matmul(Q_B[:, 0:3], tri[:, :], limc[:, :, PER - 1], start=True, stop=True).then_inc(ends_pe, 1)
                elif kind == "ends_count":
                    pe.wait_ge(ends_dve, 21)
                    for k in range(PER):
                        mm = pe.matmul(Q_B[:, 0:TILES], hot_lo[:, k, :], hot_hi[:, k, :],
                                       start=(k == 0), stop=(k == PER - 1))
                    mm.then_inc(ends_pe, 1)
                    pe.wait_ge(ends_dve, 22)
                    pe.matmul(Q_B[:, 0:TILES], trib[:, :], bmask[:, :], start=True, stop=True)
                    pe.matmul(Q_B[:, TILES:2 * TILES], onesb[:, :], bmask[:, :], start=True, stop=True,
                              skip_group_check=True).then_inc(ends_pe, 1)
                elif kind == "patch_fix":
                    pe.wait_ge(const_ready, 10)
                    pe.wait_ge(patch_dve, PER - 1)
                    pe.matmul(Y_B[0:PP, 0:D], seam[0:PP, 0:PP], CT[0:PP, PER - 1, 0:D],
                              start=True, stop=True).then_inc(patch_pe, 1)

        @block.vector
        def _(dve):
            def row_stats(st, rows):
                s, n = norm_no[st] % 3, norm_tiles(st)
                base, col = norm_cum[st] - n, norm_cols(st).start
                for u in range(n):
                    dve.bn_stats(stats[:, s, u, :], rows[u]).then_inc(stats_ready, 1)
                for u in range(n):
                    dve.wait_ge(stats_ready, base + u + 1)
                    dve.bn_aggr(mv[:, col + u, :], stats[:, s, u, :]).then_inc(mv_ready, 1)

            def normed(dst, src, st, u, done):
                s = norm_cols(st).start + u
                dve.tensor_scalar(dst, src, mv[:, s, 0:1], rs[:, s:s + 1],
                                  ALU.subtract, ALU.mult).then_inc(done, 1)

            dve.wait_ge(cols_in, 80)
            dve.reciprocal(scl[:, 2:4], scl[:, 0:2]).then_inc(scl_ready, 1)
            dve.tensor_tensor(ss[:, :], scl[:, 0:1], scl[:, 1:2], ALU.mult).then_inc(scl_ready, 1)
            for st in PLAN:
                kind, a, b = st
                if kind == "turn_w":
                    n = t_use[st]
                    dve.wait_ge(t_high, n + 1)
                    src = T_B[n % T_BANKS][:, :].rearrange("p (c e) -> p c e", c=DC)
                    if a == 3:
                        for c in range(DC):
                            i = dve.scalar_tensor_tensor(WT_l[:, a, c, :], src[:, c, :], cols[:, 2, c:c + 1],
                                                         WT_h[:, a, c, :].bitcast(F32), ALU.mult, ALU.subtract)
                        i.then_inc(t_freed, 1)
                    else:
                        dve.tensor_tensor(WT_l[:, a, :, :], src, WT_h[:, a, :, :].bitcast(F32),
                                          ALU.subtract).then_inc(t_freed, 1)
                elif kind == "xnorm":
                    dve.wait_ge(x_in[a], 16)
                    row_stats(st, [X[:, GROUP * a + u, :] for u in range(GROUP)])
                    dve.wait_ge(rs_ready, norm_no[st] + 1)
                    if a >= 1:
                        dve.wait_ge(t_filled, t_use[("turn_x", a - 1, 1)] + 1)
                    for u in range(GROUP):
                        normed(XN[:, u, :], X[:, GROUP * a + u, :], st, u, xn_ready)
                elif kind == "turn_x":
                    n = t_use[st]
                    dve.wait_ge(t_high, n + 1)
                    dve.tensor_tensor(XT_l[:, a % 2, b, :], T_B[n % T_BANKS][:, :],
                                      XT_h[:, a % 2, b, :].bitcast(F32), ALU.subtract).then_inc(t_freed, 1)
                elif kind == "turn_p":
                    n, k, w = t_use[st], p_use[(a, b)] % PT_SLOTS, P * blocks_of(a, b)
                    dve.wait_ge(t_high, n + 1)
                    dve.tensor_tensor(PT_l[:, k, 0:w], T_B[n % T_BANKS][:, 0:w],
                                      PT_h[:, k, 0:w].bitcast(F32), ALU.subtract).then_inc(t_freed, 1)
                elif kind == "proj":
                    n = s_use[st]
                    src = S_B[n % S_BANKS][:, :]
                    dve.wait_ge(s_high, high_no[st] + 1)
                    if b < 4:
                        part = (q_part, k_part)[b // 2]
                        dve.scalar_tensor_tensor(part(1, a)[:, b % 2, :], src, cols[:, b // 2, b % 2:b % 2 + 1],
                                                 part(0, a)[:, b % 2, :].bitcast(F32), ALU.add,
                                                 ALU.subtract).then_inc(s_freed, 1)
                    else:
                        t = GROUP * a + 2 * (b - 4)
                        dve.tensor_tensor(V[:, t:t + 2, 1, :], src.rearrange("p (t d) -> p t d", t=2),
                                          V[:, t:t + 2, 0, :].bitcast(F32), ALU.subtract).then_inc(s_freed, 1)
                elif kind == "score":
                    n, w = s_use[st], P * blocks_of(a, b)
                    dve.wait_ge(s_filled, n + 1)
                    if a < 2:
                        dve.wait_ge(t_filled, t_use[("turn_w", 3, 0)] + 1)
                    if a >= 2:
                        dve.wait_ge(t_filled, t_use[("turn_p", a - 2, chunks_of(a - 2) - 1)] + 1)
                    dve.tensor_scalar(SC[:, a % 2, b * 512:b * 512 + w], S_B[n % S_BANKS][:, 0:w], -SCALE, None,
                                      ALU.mult, ALU.min, accum_out=cmin[:, a % 2, b:b + 1]).then_inc(s_freed, 1)
                elif kind == "soft":
                    n = chunks_of(a)
                    dve.wait_ge(s_freed, s_use[("score", a, n - 1)] + 1)
                    if a >= 2:
                        dve.wait_ge(probs_ready, a - 1)
                    dve.tensor_reduce(nmax[:, a % 2:a % 2 + 1], cmin[:, a % 2, 0:n], AX.X, ALU.min).then_inc(min_ready, 1)
                elif kind == "attn_out":
                    dve.wait_ge(olow_added, a + 1)
                    dve.scalar_tensor_tensor(X[:, a, :], O_B[:, 0:D], rl[:, a % 2:a % 2 + 1], X[:, a, :],
                                             ALU.mult, ALU.add).then_inc(x1_ready, 1)
                    dve.wait_ge(x1_ready, a + 1)
                    row_stats(st, [X[:, a, :]])
                elif kind == "y":
                    dve.wait_ge(rs_ready, norm_no[("attn_out", a, 0)] + 1)
                    if a == 0:
                        dve.wait_ge(table_stored, 32)
                    if a >= 2:
                        dve.wait_ge(yt_filled, a - 1)
                    normed(Y[:, a % 2, :], X[:, a, :], ("attn_out", a, 0), 0, y_ready)
                elif kind == "turn_y":
                    dve.wait_ge(yt_high, a + 1)
                    dve.tensor_tensor(YT_l[:, :, :], Y_B[:, 0:D].rearrange("p (c r) -> p c r", c=DC),
                                      YT_h[:, :, :].bitcast(F32), ALU.subtract).then_inc(yt_low, 1)
                elif kind == "h":
                    dve.wait_ge(h_done, a + 1)
                    dve.wait_ge(patches_added, a + 1)
                    dve.tensor_tensor(X[:, a, :], Y_B[:, 0:D], X[:, a, :], ALU.add).then_inc(x2_ready, 1)
                    dve.wait_ge(x2_ready, a + 1)
                    row_stats(st, [X[:, a, :]])
                elif kind == "z":
                    s = a % 2
                    dve.wait_ge(rs_ready, norm_no[("h", a, 0)] + 1)
                    normed(Z[:, s, :], X[:, a, :], ("h", a, 0), 0, z_ready)
                    dve.wait_ge(scl_ready, 2)
                    dve.wait_ge(z_ready, a + 1)
                    if a >= 2:
                        dve.wait_ge(q_ready, a - 1)
                    dve.tensor_scalar(VV[:, s, :], Z[:, s, :], scl[:, 2:3], None, ALU.mult).then_inc(v_ready, 1)
                    dve.tensor_reduce(zmax[:, s:s + 1], Z[:, s, :], AX.X, ALU.max,
                                      apply_absolute_value=True).then_inc(z_ready_max, 1)
                    dve.wait_ge(v_ready, a + 1)
                    dve.tensor_scalar(MG[:, s, :].bitcast(I32), VV[:, s, :].bitcast(I32), 0x7F800000, None,
                                      ALU.bitwise_and).then_inc(bits_ready, 1)
                    dve.wait_ge(z_ready_max, a + 1)
                    dve.tensor_scalar(zmax[:, s:s + 1], zmax[:, s:s + 1], scl[:, 2:3], None,
                                      ALU.mult).then_inc(z_scaled, 1)
                    dve.wait_ge(bits_ready, a + 1)
                    dve.tensor_scalar(MG[:, s, :], MG[:, s, :], 2.0 ** -6, 1.5 * 2.0 ** 20,
                                      ALU.max, ALU.mult).then_inc(magic_ready, 1)
                    if a >= 2:
                        dve.wait_ge(f_ready, a - 1)
                    dve.wait_ge(z_scaled, a + 1)
                    dve.tensor_scalar(nanf[:, s, 0:1], zmax[:, s:s + 1], E4M3_MAX, 3.0e38, ALU.is_gt,
                                      ALU.mult).then_inc(nan_step, 1)
                    dve.wait_ge(nan_step, 2 * a + 1)
                    dve.tensor_scalar(nanf[:, s, 1:2], nanf[:, s, 0:1], 1.0e10, 0.0, ALU.mult,
                                      ALU.mult).then_inc(nan_step, 1)
                elif kind == "quant_k":
                    dve.wait_ge(kern_in, 16)
                    dve.wait_ge(scl_ready, 2)
                    dve.tensor_scalar(kv[:, :, :], kraw[:, :, :], scl[:, 3:4], None, ALU.mult).then_inc(kq_step, 1)
                    dve.wait_ge(kq_step, 1)
                    dve.tensor_scalar(km[:, :, :].bitcast(I32), kv[:, :, :].bitcast(I32), 0x7F800000, None,
                                      ALU.bitwise_and).then_inc(kq_step, 1)
                    dve.wait_ge(kq_step, 2)
                    dve.tensor_scalar(km[:, :, :], km[:, :, :], 2.0 ** -6, 1.5 * 2.0 ** 20, ALU.max,
                                      ALU.mult).then_inc(kq_step, 1)
                elif kind == "ends_sum":
                    dve.wait_ge(kq_pool, 2)
                    dve.tensor_scalar(km[:, :, :], kv[:, :, :], 3.4028e38 / E4M3_MAX, None,
                                      ALU.mult).then_inc(kq_step, 1)
                    dve.wait_ge(kq_step, 4)
                    dve.tensor_tensor(km[:, :, :], km[:, :, :], km[:, :, :], ALU.subtract).then_inc(kq_step, 1)
                    dve.wait_ge(kq_step, 5)
                    dve.tensor_tensor(kq[:, :, :], kv[:, :, :], km[:, :, :], ALU.add).then_inc(kq_ready, 1)
                    dve.wait_ge(lens_in, 32)
                    dve.tensor_scalar(limb[:, 0, :], ln[:, :], 2047, None, ALU.bitwise_and).then_inc(ends_dve, 1)
                    dve.tensor_scalar(limb[:, 1, :], ln[:, :], 11, 2047, ALU.logical_shift_right,
                                      ALU.bitwise_and).then_inc(ends_dve, 1)
                    dve.tensor_scalar(limb[:, 2, :], ln[:, :], 22, 1023, ALU.logical_shift_right,
                                      ALU.bitwise_and).then_inc(ends_dve, 1)
                    dve.wait_ge(ends_dve, 3)
                    dve.tensor_copy(limf[:, :, :], limb[:, :, :]).then_inc(ends_conv, 1)
                    dve.wait_ge(ends_conv, 1)
                    for m in range(3):
                        dve.tensor_tensor_scan(limc[:, m, :], onef[:, 0:PER], limf[:, m, :], 0.0, ALU.mult,
                                               ALU.add).then_inc(ends_dve, 1)
                    dve.wait_ge(ends_pe, 1)
                    dve.tensor_copy(limp[:, :], Q_B[:, 0:3]).then_inc(ends_dve, 1)
                    dve.wait_ge(ends_dve, 7)
                    for m in range(3):
                        dve.tensor_scalar(limt[:, m, :], limc[:, m, :], limp[:, m:m + 1], -1.0 if m == 0 else 0.0,
                                          ALU.add, ALU.add).then_inc(ends_conv, 1)
                    dve.wait_ge(ends_conv, 4)
                    dve.tensor_scalar(limt[:, 1, :], limt[:, 1, :], 11, None, ALU.logical_shift_left).then_inc(ends_dve, 1)
                    dve.tensor_scalar(limt[:, 2, :], limt[:, 2, :], 22, None, ALU.logical_shift_left).then_inc(ends_dve, 1)
                    dve.tensor_copy(endf[:, 2, :], onef[:, 0:PER]).then_inc(ends_dve, 1)
                    dve.tensor_copy(endf[:, 3, :], onef[:, 0:PER]).then_inc(ends_dve, 1)
                elif kind == "ends_place":
                    dve.wait_ge(ends_pool, 2)
                    dve.tensor_scalar(endi[:, 1, :], endi[:, 0, :], P - 1, None, ALU.bitwise_and).then_inc(ends_dve, 1)
                    dve.tensor_scalar(endi[:, 2, :], endi[:, 0, :], int(math.log2(P)), TILES - 1,
                                      ALU.logical_shift_right, ALU.bitwise_and).then_inc(ends_dve, 1)
                    dve.wait_ge(ends_dve, 13)
                    dve.tensor_copy(endf[:, 0:3, :], endi[:, 0:3, :]).then_inc(ends_dve, 1)
                    dve.wait_ge(ends_dve, 14)
                    dve.tensor_scalar(endf[:, 3, :], endf[:, 0, :], float(S - 1), 100.0, ALU.is_gt,
                                      ALU.mult).then_inc(ends_dve, 1)
                    dve.tensor_scalar(endf[:, 0, :], endf[:, 0, :], float(-S), 100.0, ALU.is_lt,
                                      ALU.mult).then_inc(ends_dve, 1)
                    dve.wait_ge(ends_dve, 16)
                    dve.tensor_tensor(endf[:, 2, :], endf[:, 2, :], endf[:, 3, :], ALU.add).then_inc(ends_dve, 1)
                    dve.wait_ge(ends_dve, 17)
                    dve.tensor_tensor(endf[:, 2, :], endf[:, 2, :], endf[:, 0, :], ALU.add).then_inc(ends_dve, 1)
                    dve.wait_ge(const_ready, 10)
                    dve.tensor_tensor(hot_lo[:, :, :], iota[:, None, :].to_broadcast((P, PER, P)),
                                      endf[:, 1, :, None].to_broadcast((P, PER, P)), ALU.is_equal).then_inc(ends_dve, 1)
                    dve.wait_ge(ends_dve, 18)
                    dve.tensor_tensor(hot_hi[:, :, :], iota[:, None, 0:TILES].to_broadcast((P, PER, TILES)),
                                      endf[:, 2, :, None].to_broadcast((P, PER, TILES)),
                                      ALU.is_equal).then_inc(ends_dve, 2)
                elif kind == "ends_count":
                    dve.wait_ge(ends_pe, 2)
                    dve.tensor_scalar(bmask[:, :], Q_B[:, 0:TILES], 1.0, None, ALU.min).then_inc(ends_dve, 1)
                    dve.wait_ge(ends_pe, 3)
                    dve.tensor_copy(btot[:, 0:2, :], Q_B[:, 0:2 * TILES].rearrange("p (a t) -> p a t", a=2)).then_inc(ends_dve, 1)
                    dve.wait_ge(ends_dve, 23)
                    dve.tensor_tensor_scan(btot[:, 2, :], onef[:, 0:TILES], btot[:, 1, :], 0.0, ALU.mult,
                                           ALU.add).then_inc(ends_dve, 1)
                    dve.tensor_tensor(btot[:, 3, :], btot[:, 0, :], btot[:, 1, :], ALU.subtract).then_inc(ends_dve, 1)
                    dve.wait_ge(ends_dve, 25)
                    dve.scalar_tensor_tensor(btot[:, 0, :], btot[:, 2, :], -1.0, btot[:, 3, :], ALU.add,
                                             ALU.add).then_inc(ends_dve, 1)
                    dve.wait_ge(ends_dve, 26)
                    dve.tensor_scalar(plug[:, :], btot[:, 0, :], 0.0, float(NPATCH - 1), ALU.max,
                                      ALU.min).then_inc(ends_dve, 1)
                elif kind == "patch_scan":
                    dve.wait_ge(patch_u, 1)
                    for k in range(1, PER):
                        dve.wait_ge(patch_u, k + 1)
                        if k >= 2:
                            dve.wait_ge(patch_dve, k - 1)
                        dve.scalar_tensor_tensor(CT[0:PP, k, 0:D], CT[0:PP, k - 1, 0:D], PATCH_A, CT[0:PP, k, 0:D],
                                                 ALU.mult, ALU.add).then_inc(patch_dve, 1)
                elif kind == "patch_fix":
                    dve.wait_ge(carry_ready, 1)
                    dve.wait_ge(patch_dve, PER - 1)
                    for k in range(PER):
                        i = dve.scalar_tensor_tensor(CT[0:PP, k, 0:D], carry[0:PP, :], PATCH_A ** (k + 1),
                                                     CT[0:PP, k, 0:D], ALU.mult, ALU.add)
                        i.then_inc(patch_dve, 1 if k < PER - 1 else 2)
                elif kind == "pv" and b == chunks_of(a) - 1:
                    dve.wait_ge(probs_ready, a + 1)
                    if a >= 2:
                        dve.wait_ge(olow_ready, a - 1)
                    dve.reciprocal(rl[:, a % 2:a % 2 + 1], lsum[:, a % 2:a % 2 + 1]).then_inc(rl_ready, 1)


_INS = ["x", "ctx_2048", "mask_BxS2_if0", "L0_attn_Wq", "L0_attn_bq", "L0_attn_Wk", "L0_attn_bk",
        "L0_attn_Wv", "L0_attn_bv", "L0_xattn_W_in", "L0_xattn_b_in", "L0_xattn_g_res", "L0_xattn_g_init",
        "L0_ffn_kernel", "L0_ffn_input_scale", "L0_ffn_kernel_scale", "L0_ffn_bias"]


def kernel(**inputs):
    import numpy as _np
    import concourse.bacc as _bacc
    from concourse import mybir as _mybir
    from concourse.bass_utils import run_bass_kernel_spmd as _run

    nc = _bacc.Bacc("TRN2", target_bir_lowering=False, num_devices=1)
    arrays, args = {}, []
    for name in _INS:
        a = _np.ascontiguousarray(inputs[name])
        arrays[f"in_{name}_dram"] = a
        args.append(nc.dram_tensor(f"in_{name}_dram", a.shape, _mybir.dt.from_np(a.dtype), kind="ExternalInput").ap())
    patches = inputs["ctx_2048"].shape[1]
    rows = inputs["x"].shape
    args.append(nc.dram_tensor("patch_table", (patches, rows[2]), F32, kind="Internal").ap())
    args.append(nc.dram_tensor("out_0_dram", rows, F32, kind="ExternalOutput").ap())
    decoder_layer(nc, *args)
    r = _run(nc, [arrays], core_ids=[0])
    return r.results[0]["out_0_dram"]
```

```python
from contextlib import ExitStack
import math

import concourse.bass as bass
from concourse import mybir

F32 = mybir.dt.float32
F32R = mybir.dt.float32r
BF16 = mybir.dt.bfloat16
I32 = mybir.dt.int32
ALU = mybir.AluOpType
ACT = mybir.ActivationFunctionType
AX = mybir.AxisListType

P = 128
LN_EPS = 1e-5
RMS_EPS = 1e-5
PATCH_EPS = 0.001
PATCH_B = math.exp(-PATCH_EPS)
PATCH_A = -math.expm1(-PATCH_EPS)
E4M3_MAX = 464.0
MASKED = -3.0e38
GROUP = 4
S_BANKS = 3
T_BANKS = 2
SLOTS = 10
AT = {"score": (0, 0, 0, 2.2), "least": 4.4, "exp": (10.1, 10.2, 10.4, 14.0),
      "turn_p": (11.8, 12.8, 13.8, 15.8), "pv": (15.2, 17, 17.5, 18.5), "attn_out": 18.8, "y": 20.8,
      "turn_y": 22.8, "h": 25.3, "x2": 25.6, "z": 28.0, "bits": 28.7, "turn_q": 32.2, "ffn": 36.0,
      "store": 37.8, "gather": 13.5}
FIRST_BEHIND = 61
BEHIND_PACE = 5
FILLERS = [4, 6, 5, 3, 3, 1, 2]
FILL_FROM = 2.7
SIDE = {"square": (1, 14), "weigh": (16, 28), "run": (17, 31.5), "fix": (37.5, 49), "quant": (0.5, 16),
      "sum": (14.5, 24), "count": (25, 37)}
TAIL = 2
PT_SLOTS = 3


def chunks_of(i):
    return i // GROUP + 1


def blocks_of(i, j):
    return min(GROUP, i + 1 - GROUP * j)


def make_plan(tiles, per):
    groups = tiles // GROUP
    plan = [("turn_w", 0, 0)] + [("xstat", u, 0) for u in range(GROUP)] + [("xroot", 0, 0)]
    plan += [("turn_w", 1, 0), ("turn_w", 2, 0)] + [("xn", u, 0) for u in range(GROUP)]
    plan += [("turn_x", 0, 0), ("turn_x", 0, 1)]
    ahead = [[("xstat", GROUP, 0), ("xstat", GROUP + 1, 0)], [("xstat", GROUP + 2, 0), ("xstat", GROUP + 3, 0)],
             [("xroot", 1, 0), ("turn_w", 3, 0)], [("xn", GROUP, 0), ("xn", GROUP + 1, 0)],
             [("xn", GROUP + 2, 0), ("xn", GROUP + 3, 0)], []]
    for m in range(6):
        plan += [("proj", 0, m)] + ahead[m]

    slots = {}

    def put(turn, slot, step):
        slots.setdefault(turn * SLOTS + slot, []).append(step)

    for t in range(tiles):
        for j in range(chunks_of(t)):
            for kind in ("score", "exp", "turn_p", "pv"):
                put(t, AT[kind][j], (kind, t, j))
        put(t, AT["least"], ("least", t, 0))
        put(t, AT["attn_out"], ("attn_out", t, 0))
    for b in range(tiles):
        start = max(b * SLOTS, FIRST_BEHIND + b * BEHIND_PACE)
        for kind in ("gather", "y", "turn_y", "h", "x2", "z", "bits", "turn_q", "ffn", "store"):
            put(0, start + AT[kind], (kind, b, 0))
    fill = []
    for g in range(1, groups):
        more = g + 1 < groups
        nxt = range(GROUP * (g + 1), GROUP * (g + 2))
        fill += [[("turn_x", g, 0)], [("turn_x", g, 1)]]
        for m in range(6):
            fill.append([("proj", g, m)])
            if more:
                fill[-1] += {0: [("xstat", t, 0) for t in nxt[:2]], 1: [("xstat", t, 0) for t in nxt[2:]],
                             2: [("xroot", g + 1, 0)], 3: [("xn", t, 0) for t in nxt[:2]],
                             4: [("xn", t, 0) for t in nxt[2:]]}.get(m, [])
    at = 0
    for turn, count in enumerate(FILLERS):
        for k in range(count):
            for step in fill[at]:
                put(turn, FILL_FROM + k * (SLOTS - FILL_FROM) / count, step)
            at += 1
    assert at == len(fill)
    for name, side in (
            ("square", [("square", 0, k) for k in range(per)] + [("patch_rms", 0, 0)]),
            ("weigh", [("weigh", 0, k) for k in range(per)]),
            ("run", [("run", 0, k) for k in range(per)] + [("seam", 0, 0)]),
            ("fix", [("fix", 0, k) for k in range(per)]),
            ("quant", [("quant_k", 0, 0), ("quant_k", 0, 1)]),
            ("sum", [("ends_limb", 0, 0), ("ends_sum", 0, 0), ("ends_int", 0, 0), ("ends_add", 0, 0),
                     ("ends_place", 0, 0)]),
            ("count", [("ends_hot", 0, 0), ("ends_hot", 0, 1), ("ends_count", 0, 0), ("ends_mask", 0, 0),
                       ("ends_rank", 0, 0), ("ends_index", 0, 0)])):
        first, last = SIDE[name]
        for n, step in enumerate(side):
            put(0, first + n * (last - first) / len(side), step)
    for k in sorted(slots):
        plan += slots[k]
    return plan


def decoder_layer(nc, x, ctx_in, lens, Wq, bq, Wk, bk, Wv, bv, W_in, b_in, g_res, g_init,
                  ffn_w, s_in, s_k, ffn_b, table, out):
    _, S, D = x.shape
    _, NPATCH, DG = ctx_in.shape
    TILES = S // P
    DC = D // P
    PER = -(-NPATCH // P)
    FULL = NPATCH // PER
    REST = NPATCH - FULL * PER
    PP = FULL + 1
    SCALE = 1.0 / math.sqrt(D)
    assert D == 256 and S % (P * GROUP) == 0 and 0 < REST < PER and DG == 2 * D
    PLAN = make_plan(TILES, PER)

    s_use = {st: n for n, st in enumerate(st for st in PLAN if st[0] in ("proj", "score"))}
    t_use = {st: n for n, st in enumerate(st for st in PLAN if st[0] in ("turn_w", "turn_x", "turn_p"))}
    p_use = {st[1:]: n for n, st in enumerate(st for st in PLAN if st[0] == "turn_p")}
    e_use = {st[1:]: n for n, st in enumerate(st for st in PLAN if st[0] == "exp")}
    norm_no = {st: n for n, st in enumerate(st for st in PLAN if st[0] in ("xroot", "attn_out", "x2"))}
    high_no = {st: n for n, st in enumerate(st for st in PLAN if st[0] == "proj")}
    assert [st[1] for st in PLAN if st[0] == "h"] == list(range(TILES))

    x_t = x.rearrange("a (t p) d -> p (a t) d", p=P)
    out_t = out.rearrange("a (t p) d -> p (a t) d", p=P)
    ctx_rows = ctx_in.rearrange("a r d -> (a r) d")

    ctx = ExitStack()
    with ctx:
        def sb(name, shape, dt=F32):
            return ctx.enter_context(nc.sbuf_tensor(name, shape, dt))

        def bank(name):
            return ctx.enter_context(nc.psum_tensor(name, [P, 512], F32))

        def sem(name):
            return ctx.enter_context(nc.semaphore(name))

        X = sb("X", [P, TILES, D])
        XN = sb("XN", [P, GROUP, D])
        XT_h = sb("XT_h", [P, 2, DC, GROUP * P], F32R)
        XT_l = sb("XT_l", [P, 2, DC, GROUP * P], F32R)
        QT_h = sb("QT_h", [P, DC, S - GROUP * P], F32R)
        QT_l = sb("QT_l", [P, DC, S - GROUP * P], F32R)
        KT_h = sb("KT_h", [P, DC, S], F32R)
        KT_l = sb("KT_l", [P, DC, S], F32R)
        V = sb("V", [P, TILES, 2, D], F32R)
        SC = sb("SC", [P, 2, S])
        PT_h = sb("PT_h", [P, PT_SLOTS, GROUP * P], F32R)
        PT_l = sb("PT_l", [P, PT_SLOTS, GROUP * P], F32R)
        Wraw = [SC[:, 0, 512 * m:512 * m + 512].rearrange("p (b d) -> p b d", b=2) for m in range(4)]
        WT_h = sb("WT_h", [P, 4, DC, D], F32R)
        WT_l = sb("WT_l", [P, 4, DC, D], F32R)
        CT = sb("CT", [P, PER, DG])
        GB = CT[:, 0:TILES // 2, :].rearrange("p k (h d) -> p (k h) d", h=2)
        late = CT[:, TILES // 2:PER, :].rearrange("p k d -> p (k d)")
        Y, VV, MG = (late[:, 512 * n:512 * (n + 1)].rearrange("p (s d) -> p s d", s=2) for n in range(3))
        Z, Q8, F1 = (late[:, 1536 + 256 * n:1792 + 256 * n].bitcast(BF16).rearrange("p (s d) -> p s d", s=2)
                     for n in range(3))
        carry = SC[:, 0, 1024:1024 + D]
        bv_b = sb("bv_b", [P, D])
        bin_b = sb("bin_b", [P, D])
        ginit_b = sb("ginit_b", [P, D])
        fb_b = sb("fb_b", [P, D], BF16)
        cols = sb("cols", [P, 3, DC])
        scl = sb("scl", [P, 4])
        ss = sb("ss", [P, 1])
        identf = sb("identf", [P, P])
        identb = sb("identb", [P, P], BF16)
        maskb = sb("maskb", [P, P], BF16)
        tri = SC[:, 1, S - P:S]
        trib = sb("trib", [P, P], BF16)
        onesb = sb("onesb", [P, P], BF16)
        seam = sb("seam", [P, P])
        neg_half = sb("neg_half", [P, 16])
        stats = sb("stats", [P, 2, 6])
        mv = sb("mv", [P, 3 * TILES, 2])
        rs = sb("rs", [P, 3 * TILES])
        negm = sb("negm", [P, GROUP])
        shift = sb("shift", [P, GROUP])
        ve = sb("ve", [P, 3 * TILES])
        cmin = sb("cmin", [P, 2, GROUP])
        nmax = sb("nmax", [P, 2])
        lsum = sb("lsum", [P, 2, GROUP])
        lall = sb("lall", [P, 2])
        rl = sb("rl", [P, 2])
        YT_h = sb("YT_h", [P, DC, P], F32R)
        YT_l = sb("YT_l", [P, DC, P], F32R)
        zmax = sb("zmax", [P, 2])
        nanf = sb("nanf", [P, 2, 2])
        QT8 = sb("QT8", [P, DC, P], BF16)
        kraw = sb("kraw", [P, DC, D], BF16)
        kv, km = (SC[:, 0, 1024 + 512 * n:1536 + 512 * n].rearrange("p (c e) -> p c e", c=DC) for n in range(2))
        kq = sb("kq", [P, DC, D], BF16)
        ln = sb("ln", [P, PER], I32)
        limb = sb("limb", [P, 3, PER], I32)
        limf = sb("limf", [P, 3, PER])
        limc = sb("limc", [P, 3, PER])
        limp = sb("limp", [P, 3])
        limt = sb("limt", [P, 3, PER], I32)
        endi = sb("endi", [P, 4, PER], I32)
        endf = sb("endf", [P, 4, PER])
        iota = sb("iota", [P, P], BF16)
        hot_lo = SC[:, 1, S // 2:S // 2 + PER * P // 2].bitcast(BF16).rearrange("p (k r) -> p k r", r=P)
        hot_hi = sb("hot_hi", [P, PER, TILES], BF16)
        onef = sb("onef", [P, 16])
        bmask = sb("bmask", [P, TILES], BF16)
        btot = sb("btot", [P, 4, TILES])
        plug = sb("plug", [P, TILES], I32)
        ssq = sb("ssq", [P, PER])
        prs = sb("prs", [P, PER])

        S_B = [bank(f"S_B{n}") for n in range(S_BANKS)]
        T_B = [bank(f"T_B{n}") for n in range(T_BANKS)]
        O_B = bank("O_B")
        Y_B = bank("Y_B")
        Q_B = bank("Q_B")

        x_in = [sem(f"x_in{g}") for g in range(TILES // GROUP)]
        w_in = [sem(f"w_in{m}") for m in range(4)]
        cols_in = sem("cols_in")
        bin_in = sem("bin_in")
        rows_in = sem("rows_in")
        bv_in = sem("bv_in")
        scl_in = sem("scl_in")
        kern_in = sem("kern_in")
        lens_in = sem("lens_in")
        ctx_loaded = sem("ctx_loaded")
        const_ready = sem("const_ready")
        const_step = sem("const_step")
        scl_ready = sem("scl_ready")
        stats_ready = sem("stats_ready")
        mv_ready = sem("mv_ready")
        ve_ready = sem("ve_ready")
        rs_ready = sem("rs_ready")
        xn_ready = sem("xn_ready")
        negm_ready = sem("negm_ready")
        shift_ready = sem("shift_ready")
        xb_ready = sem("xb_ready")
        s_filled = sem("s_filled")
        s_high = sem("s_high")
        s_freed = sem("s_freed")
        t_filled = sem("t_filled")
        t_high = sem("t_high")
        t_freed = sem("t_freed")
        min_ready = sem("min_ready")
        probs_ready = sem("probs_ready")
        rl_ready = sem("rl_ready")
        lall_ready = sem("lall_ready")
        pv_done = sem("pv_done")
        x1_ready = sem("x1_ready")
        y_ready = sem("y_ready")
        patches_added = sem("patches_added")
        yt_filled = sem("yt_filled")
        yt_high = sem("yt_high")
        yt_low = sem("yt_low")
        h_done = sem("h_done")
        x2_ready = sem("x2_ready")
        z_ready = sem("z_ready")
        v_ready = sem("v_ready")
        z_ready_max = sem("z_ready_max")
        z_scaled = sem("z_scaled")
        bits_ready = sem("bits_ready")
        magic_ready = sem("magic_ready")
        nan_step = sem("nan_step")
        round_step = sem("round_step")
        q_ready = sem("q_ready")
        qt_filled = sem("qt_filled")
        qt_ready = sem("qt_ready")
        ffn_done = sem("ffn_done")
        f_ready = sem("f_ready")
        f_step = sem("f_step")
        out_ready = sem("out_ready")
        out_stored = sem("out_stored")
        kq_step = sem("kq_step")
        kq_pool = sem("kq_pool")
        kq_ready = sem("kq_ready")
        ends_pool = sem("ends_pool")
        ends_pe = sem("ends_pe")
        patch_sq = sem("patch_sq")
        patch_rs = sem("patch_rs")
        patch_u = sem("patch_u")
        patch_run = sem("patch_run")
        patch_fixed = sem("patch_fixed")
        patch_gained = sem("patch_gained")
        patch_whole = sem("patch_whole")
        gain_in = sem("gain_in")
        patch_pe = sem("patch_pe")
        carry_ready = sem("carry_ready")
        table_stored = sem("table_stored")
        gathered = [sem(f"gathered{t}") for t in range(TILES)]
        limbs_cut = sem("limbs_cut")
        limbs_float = sem("limbs_float")
        limbs_run = sem("limbs_run")
        limbs_before = sem("limbs_before")
        limbs_whole = sem("limbs_whole")
        limbs_shifted = sem("limbs_shifted")
        ends_split = sem("ends_split")
        ends_float = sem("ends_float")
        ends_outside = sem("ends_outside")
        ends_kept = sem("ends_kept")
        hot_ready = sem("hot_ready")
        bmask_ready = sem("bmask_ready")
        btot_ready = sem("btot_ready")
        brun_ready = sem("brun_ready")
        rank_ready = sem("rank_ready")
        plug_ready = sem("plug_ready")

        def q_part(part, g):
            if g == TILES // GROUP - 1:
                return (XT_h, XT_l)[part][:, (g - 1) % 2, :, :]
            return (QT_h, QT_l)[part][:, :, g * GROUP * P:(g + 1) * GROUP * P]

        def k_part(part, g):
            return (KT_h, KT_l)[part][:, :, g * GROUP * P:(g + 1) * GROUP * P]

        block = ctx.enter_context(nc.Block())

        def norm_cols(st):
            kind, a, _ = st
            first = {"xroot": GROUP * a, "attn_out": TILES + a, "x2": 2 * TILES + a}[kind]
            return slice(first, first + norm_tiles(st))

        def norm_tiles(st):
            return GROUP if st[0] == "xroot" else 1

        stat_no = {st: n for n, st in enumerate(st for st in PLAN if st[0] in ("xstat", "attn_out", "x2"))}

        def stats_of(st):
            return stat_no[("xstat", GROUP * st[1] + GROUP - 1, 0) if st[0] == "xroot" else st] + 1


        @block.sync
        def _(sp):
            def row(dst, src, done):
                sp.dma_start(dst, src.rearrange("(a n) -> a n", a=1).to_broadcast((P, src.shape[0]))).then_inc(done, 16)

            sp.dma_start(X[:, 0:GROUP, :], x_t[:, 0:GROUP, :]).then_inc(x_in[0], 16)
            for m, w in ((1, Wk), (2, Wv)):
                sp.dma_start(Wraw[m], w.rearrange("(b p) d -> p b d", p=P)).then_inc(w_in[m], 16)
            sp.dma_start(X[:, GROUP:2 * GROUP, :], x_t[:, GROUP:2 * GROUP, :]).then_inc(x_in[1], 16)
            sp.dma_start(Wraw[3], W_in.rearrange("(b p) d -> p b d", p=P)).then_inc(w_in[3], 16)
            row(bv_b[:, :], bv, bv_in)
            sp.dma_start(CT[0:FULL, :, :],
                         ctx_rows[0:FULL * PER, :].rearrange("(p k) d -> p k d", k=PER)).then_inc(ctx_loaded, 16)
            sp.dma_start(CT[FULL:PP, 0:REST, :],
                         ctx_rows[FULL * PER:NPATCH, :].rearrange("(p k) d -> p k d", k=REST)).then_inc(ctx_loaded, 16)
            row(ginit_b[:, :], g_init[0:D], gain_in)
            sp.dma_start(CT[FULL:PP, REST:PER, :],
                         ctx_rows[0:PER - REST, :].rearrange("(p k) d -> p k d", k=PER - REST)).then_inc(ctx_loaded, 16)
            for g in range(2, TILES // GROUP):
                sp.dma_start(X[:, g * GROUP:(g + 1) * GROUP, :],
                             x_t[:, g * GROUP:(g + 1) * GROUP, :]).then_inc(x_in[g], 16)
            sp.dma_start(kraw[:, :, :], ffn_w.rearrange("(c p) e -> p c e", p=P)).then_inc(kern_in, 16)
            row(scl[:, 0:1], s_in, scl_in)
            row(scl[:, 1:2], s_k, scl_in)
            row(bin_b[:, :], b_in, bin_in)
            row(fb_b[:, :], ffn_b, rows_in)
            sp.wait_ge(patch_whole, PER)
            sp.dma_start(table[0:FULL * PER, :].rearrange("(p k) d -> p k d", k=PER),
                         CT[0:FULL, :, 0:D]).then_inc(table_stored, 16)
            sp.dma_start(table[FULL * PER:NPATCH, :].rearrange("(p k) d -> p k d", k=REST),
                         CT[FULL:PP, 0:REST, 0:D]).then_inc(table_stored, 16)
            for b in range(TILES):
                sp.wait_ge(out_ready, b + 1)
                sp.dma_start(out_t[:, b, :], X[:, b, :]).then_inc(out_stored, 16)
            sp.wait_ge(out_stored, 16 * TILES)
            sp.wait_ge(table_stored, 32)

        def add_patches(eng, a):
            eng.wait_ge(gathered[a], 16)
            eng.wait_ge(y_ready, a + 1)
            eng.tensor_tensor(X[:, a, :], X[:, a, :], GB[:, a, :], ALU.add).then_inc(patches_added, 1)

        def round_rows(eng, a):
            s = a % 2
            eng.wait_ge(magic_ready, a + 1)
            eng.tensor_tensor(VV[:, s, :], VV[:, s, :], MG[:, s, :], ALU.add).then_inc(round_step, 1)
            eng.wait_ge(round_step, a + 1)
            if a >= 2:
                eng.wait_ge(qt_filled, a - 1)
            eng.tensor_tensor(Q8[:, s, :], VV[:, s, :], MG[:, s, :], ALU.subtract).then_inc(q_ready, 1)

        def finish_rows(eng, a):
            s = a % 2
            eng.wait_ge(rows_in, 16)
            eng.wait_ge(f_ready, a + 1)
            eng.tensor_tensor(F1[:, s, :], F1[:, s, :], fb_b[:, :], ALU.add).then_inc(f_step, 1)
            eng.wait_ge(f_step, a + 1)
            eng.tensor_tensor(X[:, a, :], X[:, a, :], F1[:, s, :], ALU.add).then_inc(out_ready, 1)

        @block.gpsimd
        def _(pool):
            pool.memset(identf[:, :], 0.0).then_inc(const_step, 1)
            pool.memset(identb[:, :], 0.0).then_inc(const_step, 1)
            pool.memset(maskb[:, :], 0.0).then_inc(const_step, 1)
            pool.memset(tri[:, :], 0.0).then_inc(const_step, 1)
            pool.memset(trib[:, :], 1.0).then_inc(const_step, 1)
            pool.memset(seam[:, :], 0.0).then_inc(const_step, 1)
            pool.memset(onesb[:, :], 1.0).then_inc(const_ready, 1)
            pool.memset(neg_half[:, :], -0.5).then_inc(const_ready, 1)
            pool.memset(onef[:, :], 1.0).then_inc(const_ready, 1)
            pool.wait_ge(const_step, 6)
            for m in (identf, identb):
                pool.affine_select(out=m[:, :], in_=m[:, :], compare_op=ALU.not_equal, fill=1.0, base=0,
                                   pattern=[[-1, P]], channel_multiplier=1).then_inc(const_ready, 1)
            pool.affine_select(out=maskb[:, :], in_=maskb[:, :], compare_op=ALU.is_ge, fill=MASKED, base=0,
                               pattern=[[-1, P]], channel_multiplier=1).then_inc(const_ready, 1)
            pool.wait_ge(const_ready, 5)
            pool.memset(ln[:, :], 0).then_inc(const_step, 1)
            pool.affine_select(out=tri[:, :], in_=tri[:, :], compare_op=ALU.is_ge, fill=1.0, base=0,
                               pattern=[[-1, P]], channel_multiplier=1).then_inc(const_ready, 1)
            pool.affine_select(out=trib[:, :], in_=trib[:, :], compare_op=ALU.is_ge, fill=0.0, base=0,
                               pattern=[[1, P]], channel_multiplier=-1).then_inc(const_ready, 1)
            pool.affine_select(out=seam[:, :], in_=seam[:, :], compare_op=ALU.not_equal, fill=1.0, base=1,
                               pattern=[[-1, P]], channel_multiplier=1).then_inc(const_step, 1)
            pool.wait_ge(const_step, 8)
            pool.affine_select(out=seam[:, :], in_=seam[:, :], compare_op=ALU.not_equal,
                               fill=PATCH_A ** PER, base=2,
                               pattern=[[-1, P]], channel_multiplier=1).then_inc(const_ready, 1)
            pool.iota(iota[:, :], pattern=[[1, P]], base=0, channel_multiplier=0,
                      allow_small_or_imprecise_dtypes=True).then_inc(const_ready, 1)
            pool.dma_start(ln[0:FULL, :], lens[0, 0:FULL * PER].rearrange("(p k) -> p k", k=PER)).then_inc(lens_in, 16)
            pool.dma_start(ln[FULL:PP, 0:REST],
                           lens[0, FULL * PER:NPATCH].rearrange("(p k) -> p k", k=REST)).then_inc(lens_in, 16)

            def rsqrt_of_var(st, mul, add):
                s, n, no = norm_cols(st), norm_tiles(st), norm_no[st]
                pool.wait_ge(mv_ready, stats_of(st))
                pool.tensor_scalar(ve[:, s], mv[:, s, 1], mul, add, ALU.mult, ALU.add).then_inc(ve_ready, 1)
                pool.wait_ge(ve_ready, no + 1)
                pool.tensor_tensor(rs[:, s], ve[:, s], neg_half[:, 0:n], ALU.pow).then_inc(rs_ready, 1)

            for st in PLAN:
                kind, a, b = st
                if kind == "xroot":
                    cs = norm_cols(st)
                    rsqrt_of_var(st, 1.0, LN_EPS)
                    pool.tensor_scalar(negm[:, :], mv[:, cs, 0], -1.0, 0.0, ALU.mult, ALU.add).then_inc(negm_ready, 1)
                    pool.wait_ge(rs_ready, norm_no[st] + 1)
                    pool.wait_ge(negm_ready, a + 1)
                    if a >= 1:
                        pool.wait_ge(xn_ready, GROUP * a)
                    pool.tensor_tensor(shift[:, :], negm[:, :], rs[:, cs], ALU.mult).then_inc(shift_ready, 1)
                elif kind == "xn":
                    pool.wait_ge(bv_in, 16)
                    pool.wait_ge(xn_ready, a + 1)
                    pool.tensor_tensor(X[:, a, :], X[:, a, :], bv_b[:, :], ALU.add).then_inc(xb_ready, 1)
                elif kind == "attn_out":
                    rsqrt_of_var(st, 1.0 + RMS_EPS, RMS_EPS * LN_EPS)
                elif kind == "square":
                    pool.wait_ge(gain_in, 16)
                    pool.wait_ge(patch_sq, b + 1)
                    pool.tensor_tensor(CT[0:PP, b, 0:D], CT[0:PP, b, 0:D], ginit_b[0:PP, :],
                                       ALU.mult).then_inc(patch_gained, 1)
                elif kind == "fix":
                    pool.wait_ge(bin_in, 16)
                    pool.wait_ge(patch_fixed, b + 1)
                    pool.tensor_tensor(CT[0:PP, b, 0:D], CT[0:PP, b, 0:D], bin_b[0:PP, :],
                                       ALU.add).then_inc(patch_whole, 1)
                elif kind == "turn_y" and a < TILES - TAIL:
                    add_patches(pool, a)
                elif kind == "x2":
                    rsqrt_of_var(st, 1.0, LN_EPS)
                elif kind == "bits" and a < TILES - TAIL:
                    round_rows(pool, a)
                elif kind == "store" and a < TILES - TAIL:
                    finish_rows(pool, a)
                elif kind == "quant_k" and b == 0:
                    pool.wait_ge(kq_step, 3)
                    pool.tensor_tensor(kv[:, :, :], kv[:, :, :], km[:, :, :], ALU.add).then_inc(kq_pool, 1)
                    pool.wait_ge(kq_pool, 1)
                    pool.tensor_tensor(kv[:, :, :], kv[:, :, :], km[:, :, :], ALU.subtract).then_inc(kq_pool, 1)
                elif kind == "ends_add":
                    pool.wait_ge(limbs_shifted, 2)
                    pool.tensor_tensor(endi[:, 0, :], limt[:, 0, :], limt[:, 1, :], ALU.add).then_inc(ends_pool, 1)
                    pool.wait_ge(ends_pool, 1)
                    pool.tensor_tensor(endi[:, 0, :], endi[:, 0, :], limt[:, 2, :], ALU.add).then_inc(ends_pool, 1)
                elif kind == "patch_rms":
                    pool.wait_ge(patch_sq, PER)
                    pool.tensor_scalar(prs[0:PP, :], ssq[0:PP, :], 1.0 / DG, RMS_EPS, ALU.mult, ALU.add).then_inc(patch_rs, 1)
                    pool.wait_ge(patch_rs, 1)
                    pool.tensor_tensor(prs[0:PP, :], prs[0:PP, :], neg_half[0:PP, 0:PER], ALU.pow).then_inc(patch_rs, 1)
                    pool.wait_ge(patch_rs, 2)
                    pool.tensor_scalar(prs[0:PP, :], prs[0:PP, :], PATCH_B, 0.0, ALU.mult, ALU.add).then_inc(patch_rs, 1)
                elif kind == "gather":
                    pool.wait_ge(table_stored, 32)
                    pool.wait_ge(plug_ready, 1)
                    pool.indirect_dma_start(GB[:, a, :], None, table[:, :],
                                            bass.IndirectOffsetOnAxis(plug[:, a:a + 1].bitcast(mybir.dt.uint32), 0),
                                            bounds_check=NPATCH - 1).then_inc(gathered[a], 16)

        @block.scalar
        def _(act):
            act.dma_start(Wraw[0], Wq.rearrange("(b p) d -> p b d", p=P)).then_inc(w_in[0], 16)
            for n, col in enumerate((bq, bk, g_res)):
                act.dma_start(cols[:, n, :], col.rearrange("(c p) -> p c", p=P),
                              allow_slow_non_contiguous=True).then_inc(cols_in, 16)

            for st in PLAN:
                kind, a, b = st
                if kind == "turn_w":
                    n = t_use[st]
                    act.wait_ge(t_filled, n + 1)
                    src = T_B[n % T_BANKS][:, :].rearrange("p (c e) -> p c e", c=DC)
                    if a == 3:
                        act.wait_ge(cols_in, 48)
                        act.activation(WT_h[:, a, 0, :], src[:, 0, :], ACT.Copy, scale=cols[:, 2, 0:1])
                        act.activation(WT_h[:, a, 1, :], src[:, 1, :], ACT.Copy,
                                       scale=cols[:, 2, 1:2]).then_inc(t_high, 1)
                    else:
                        act.activation(WT_h[:, a, :, :], src, ACT.Copy).then_inc(t_high, 1)
                elif kind == "xn":
                    g, u = a // GROUP, a % GROUP
                    act.wait_ge(shift_ready, g + 1)
                    if g >= 1:
                        act.wait_ge(t_filled, t_use[("turn_x", g - 1, 1)] + 1)
                    act.activation(XN[:, u, :], X[:, a, :], ACT.Identity, bias=shift[:, u:u + 1],
                                   scale=rs[:, a:a + 1]).then_inc(xn_ready, 1)
                elif kind == "turn_x":
                    n = t_use[st]
                    act.wait_ge(t_filled, n + 1)
                    if a >= 2:
                        act.wait_ge(s_filled, s_use[("proj", a - 2, 5)] + 1)
                    act.activation(XT_h[:, a % 2, b, :], T_B[n % T_BANKS][:, :], ACT.Copy).then_inc(t_high, 1)
                elif kind == "turn_p":
                    n, k, w = t_use[st], p_use[(a, b)], P * blocks_of(a, b)
                    act.wait_ge(t_filled, n + 1)
                    if k >= PT_SLOTS:
                        act.wait_ge(pv_done, k - PT_SLOTS + 1)
                    act.activation(PT_h[:, k % PT_SLOTS, 0:w], T_B[n % T_BANKS][:, 0:w], ACT.Copy).then_inc(t_high, 1)
                elif kind == "proj":
                    n = s_use[st]
                    act.wait_ge(s_filled, n + 1)
                    src = S_B[n % S_BANKS][:, :]
                    if b < 4:
                        act.wait_ge(cols_in, 48)
                        dst = (q_part, k_part)[b // 2](0, a)[:, b % 2, :]
                        act.activation(dst, src, ACT.Identity, bias=cols[:, b // 2, b % 2:b % 2 + 1]).then_inc(s_high, 1)
                    else:
                        t = GROUP * a + 2 * (b - 4)
                        act.activation(V[:, t:t + 2, 0, :], src.rearrange("p (t d) -> p t d", t=2),
                                       ACT.Copy).then_inc(s_high, 1)
                elif kind == "exp":
                    w = P * blocks_of(a, b)
                    act.wait_ge(min_ready, a + 1)
                    if a >= 2 and b == 0:
                        act.wait_ge(rl_ready, a - 1)
                    part = SC[:, a % 2, b * 512:b * 512 + w]
                    act.activation(part, part, ACT.Exp, scale=-1.0, bias=nmax[:, a % 2:a % 2 + 1],
                                   accum_out=lsum[:, a % 2, b:b + 1]).then_inc(probs_ready, 1)
                elif kind == "turn_y":
                    act.wait_ge(yt_filled, a + 1)
                    act.activation(YT_h[:, :, :], Y_B[:, 0:D].rearrange("p (c r) -> p c r", c=DC),
                                   ACT.Copy).then_inc(yt_high, 1)
                elif kind == "turn_q":
                    act.wait_ge(qt_filled, a + 1)
                    act.activation(QT8[:, :, :], Q_B[:, 0:P].bitcast(BF16).rearrange("p (c r) -> p c r", c=DC),
                                   ACT.Copy).then_inc(qt_ready, 1)
                elif kind == "ffn":
                    act.wait_ge(ffn_done, a + 1)
                    act.wait_ge(nan_step, 2 * (a + 1))
                    act.wait_ge(scl_ready, 2)
                    if a >= 2:
                        act.wait_ge(out_ready, a - 1)
                    act.activation(F1[:, a % 2, :], Q_B[:, 0:D], ACT.Identity, scale=ss[:, 0:1],
                                   bias=nanf[:, a % 2, 1:2]).then_inc(f_ready, 1)
                elif kind == "square":
                    act.wait_ge(ctx_loaded, 48)
                    if b >= 2:
                        act.wait_ge(patch_sq, b - 1)
                    act.activation((Q_B, Y_B)[b % 2][0:PP, :], CT[0:PP, b, :], ACT.Square,
                                   accum_out=ssq[0:PP, b:b + 1]).then_inc(patch_sq, 1)
                elif kind == "weigh":
                    act.wait_ge(patch_rs, 3)
                    act.wait_ge(patch_gained, b + 1)
                    act.activation(CT[0:PP, b, 0:D], CT[0:PP, b, 0:D], ACT.Copy,
                                   scale=prs[0:PP, b:b + 1]).then_inc(patch_u, 1)
                elif kind == "seam":
                    act.wait_ge(patch_pe, 1)
                    act.activation(carry[0:PP, :], Y_B[0:PP, 0:D], ACT.Copy).then_inc(carry_ready, 1)
                elif kind == "z":
                    act.wait_ge(z_ready, a + 1)
                    act.wait_ge(scl_ready, 2)
                    if a >= 2:
                        act.wait_ge(q_ready, a - 1)
                    act.activation(VV[:, a % 2, :], Z[:, a % 2, :], ACT.Copy, scale=scl[:, 2:3]).then_inc(v_ready, 1)

        @block.tensor
        def _(pe):
            pe.wait_ge(const_ready, 6)

            def three_pass(ps, st_h, st_l, mv_h, mv_l, first, last):
                pe.matmul(ps, st_h, mv_h, start=first, stop=False)
                pe.matmul(ps, st_h, mv_l, start=False, stop=False)
                return pe.matmul(ps, st_l, mv_h, start=False, stop=last)

            def take_s(st):
                n = s_use[st]
                if n >= S_BANKS:
                    pe.wait_ge(s_freed, n - S_BANKS + 1)
                return S_B[n % S_BANKS]

            def take_t(st):
                n = t_use[st]
                if n >= T_BANKS:
                    pe.wait_ge(t_freed, n - T_BANKS + 1)
                return T_B[n % T_BANKS]

            for st in PLAN:
                kind, a, b = st
                if kind == "turn_w":
                    pe.wait_ge(w_in[a], 16)
                    ps = take_t(st)
                    for c in range(DC):
                        for e in range(DC):
                            mm = pe.transpose(ps[:, c * D + e * P:c * D + (e + 1) * P],
                                              Wraw[a][:, e, c * P:(c + 1) * P], identf[:, :])
                    mm.then_inc(t_filled, 1)
                elif kind == "turn_x":
                    pe.wait_ge(xn_ready, GROUP * (a + 1))
                    ps = take_t(st)
                    for t in range(GROUP):
                        mm = pe.transpose(ps[:, t * P:(t + 1) * P], XN[:, t, b * P:(b + 1) * P], identf[:, :])
                    mm.then_inc(t_filled, 1)
                elif kind == "proj":
                    pe.wait_ge(t_freed, t_use[("turn_x", a, 1)] + 1)
                    pe.wait_ge(t_freed, t_use[("turn_w", b // 2, 0)] + 1)
                    ps, g = take_s(st), a % 2
                    if b < 4:
                        w, e = b // 2, slice((b % 2) * P, (b % 2 + 1) * P)
                        for c in range(DC):
                            mm = three_pass(ps[:, :], WT_h[:, w, c, e], WT_l[:, w, c, e],
                                            XT_h[:, g, c, :], XT_l[:, g, c, :], c == 0, c == DC - 1)
                    else:
                        for u in range(2):
                            r = slice((2 * (b - 4) + u) * P, (2 * (b - 4) + u + 1) * P)
                            for c in range(DC):
                                mm = three_pass(ps[:, u * D:(u + 1) * D], XT_h[:, g, c, r], XT_l[:, g, c, r],
                                                WT_h[:, 2, c, :], WT_l[:, 2, c, :], c == 0, c == DC - 1)
                    mm.then_inc(s_filled, 1)
                elif kind == "score":
                    for g, m in ((a // GROUP, 1), (b, 3)):
                        pe.wait_ge(s_freed, s_use[("proj", g, m)] + 1)
                    ps, n = take_s(st), blocks_of(a, b)
                    g, r = a // GROUP, slice(a % GROUP * P, (a % GROUP + 1) * P)
                    diagonal = b == chunks_of(a) - 1
                    for c in range(DC):
                        mm = three_pass(ps[:, 0:n * P], q_part(0, g)[:, c, r], q_part(1, g)[:, c, r],
                                        k_part(0, b)[:, c, 0:n * P], k_part(1, b)[:, c, 0:n * P],
                                        c == 0, c == DC - 1 and not diagonal)
                    if diagonal:
                        mm = pe.matmul(ps[:, (n - 1) * P:n * P], identb[:, :], maskb[:, :], start=False, stop=True)
                    mm.then_inc(s_filled, 1)
                elif kind == "turn_p":
                    pe.wait_ge(probs_ready, e_use[(a, b)] + 1)
                    ps = take_t(st)
                    for u in range(blocks_of(a, b)):
                        k = (b * GROUP + u) * P
                        mm = pe.transpose(ps[:, u * P:(u + 1) * P], SC[:, a % 2, k:k + P], identf[:, :])
                    mm.then_inc(t_filled, 1)
                elif kind == "pv":
                    pe.wait_ge(t_freed, t_use[("turn_p", a, b)] + 1)
                    if b == 0:
                        if a >= 1:
                            pe.wait_ge(x1_ready, a)
                    slot, n = p_use[(a, b)] % PT_SLOTS, blocks_of(a, b)
                    pe.wait_ge(s_freed, s_use[("proj", b, 5)] + 1 if n > 2 else s_use[("proj", b, 4)] + 1)
                    for u in range(n):
                        t, r = b * GROUP + u, slice(u * P, (u + 1) * P)
                        mm = three_pass(O_B[:, 0:D], PT_h[:, slot, r], PT_l[:, slot, r], V[:, t, 0, :], V[:, t, 1, :],
                                        t == 0, t == a)
                    mm.then_inc(pv_done, 1)
                elif kind == "turn_y":
                    pe.wait_ge(y_ready, a + 1)
                    if a == 0:
                        pe.wait_ge(carry_ready, 1)
                    if a >= 1:
                        pe.wait_ge(x2_ready, a)
                    for c in range(DC):
                        mm = pe.transpose(Y_B[:, c * P:(c + 1) * P], Y[:, a % 2, c * P:(c + 1) * P], identf[:, :])
                    mm.then_inc(yt_filled, 1)
                elif kind == "h":
                    pe.wait_ge(yt_low, a + 1)
                    pe.wait_ge(t_freed, t_use[("turn_w", 3, 0)] + 1)
                    for c in range(DC):
                        mm = three_pass(Y_B[:, 0:D], YT_h[:, c, :], YT_l[:, c, :], WT_h[:, 3, c, :], WT_l[:, 3, c, :],
                                        c == 0, c == DC - 1)
                    mm.then_inc(h_done, 1)
                elif kind == "turn_q":
                    pe.wait_ge(q_ready, a + 1)
                    if a >= 1:
                        pe.wait_ge(f_ready, a)
                    if a == 0:
                        pe.wait_ge(btot_ready, 1)
                    for c in range(DC):
                        mm = pe.transpose(Q_B[:, 0:P].bitcast(BF16)[:, c * P:(c + 1) * P],
                                          Q8[:, a % 2, c * P:(c + 1) * P], identb[:, :])
                    mm.then_inc(qt_filled, 1)
                elif kind == "ffn":
                    pe.wait_ge(qt_ready, a + 1)
                    pe.wait_ge(kq_ready, 1)
                    for c in range(DC):
                        mm = pe.matmul(Q_B[:, 0:D], QT8[:, c, :], kq[:, c, :], start=(c == 0), stop=(c == DC - 1))
                    mm.then_inc(ffn_done, 1)
                elif kind == "ends_sum":
                    pe.wait_ge(const_ready, 10)
                    pe.wait_ge(patch_sq, PER)
                    pe.wait_ge(limbs_run, 3)
                    pe.matmul(Q_B[:, 0:3], tri[:, :], limc[:, :, PER - 1], start=True, stop=True).then_inc(ends_pe, 1)
                elif kind == "ends_count":
                    pe.wait_ge(hot_ready, 3)
                    pe.wait_ge(limbs_before, 1)
                    for k in range(PER):
                        mm = pe.matmul(Q_B[:, 0:TILES], hot_lo[:, k, :], hot_hi[:, k, :],
                                       start=(k == 0), stop=(k == PER - 1))
                    mm.then_inc(ends_pe, 1)
                elif kind == "ends_rank":
                    pe.wait_ge(bmask_ready, 1)
                    pe.matmul(Q_B[:, 0:TILES], trib[:, :], bmask[:, :], start=True, stop=True)
                    pe.matmul(Q_B[:, TILES:2 * TILES], onesb[:, :], bmask[:, :], start=True, stop=True,
                              skip_group_check=True).then_inc(ends_pe, 1)
                elif kind == "seam":
                    pe.wait_ge(const_ready, 10)
                    pe.wait_ge(patch_run, PER - 1)
                    pe.matmul(Y_B[0:PP, 0:D], seam[0:PP, 0:PP], CT[0:PP, PER - 1, 0:D],
                              start=True, stop=True).then_inc(patch_pe, 1)

        @block.vector
        def _(dve):
            def row_stats(st, row, col):
                no = stat_no[st]
                dve.bn_stats(stats[:, no % 2, :], row).then_inc(stats_ready, 1)
                dve.wait_ge(stats_ready, no + 1)
                dve.bn_aggr(mv[:, col, :], stats[:, no % 2, :]).then_inc(mv_ready, 1)

            def normed(dst, src, st, u, done):
                s = norm_cols(st).start + u
                dve.tensor_scalar(dst, src, mv[:, s, 0:1], rs[:, s:s + 1],
                                  ALU.subtract, ALU.mult).then_inc(done, 1)

            for st in PLAN:
                kind, a, b = st
                if kind == "turn_w":
                    n = t_use[st]
                    dve.wait_ge(t_high, n + 1)
                    src = T_B[n % T_BANKS][:, :].rearrange("p (c e) -> p c e", c=DC)
                    if a == 3:
                        dve.wait_ge(cols_in, 48)
                        for c in range(DC):
                            i = dve.scalar_tensor_tensor(WT_l[:, a, c, :], src[:, c, :], cols[:, 2, c:c + 1],
                                                         WT_h[:, a, c, :].bitcast(F32), ALU.mult, ALU.subtract)
                        i.then_inc(t_freed, 1)
                    else:
                        dve.tensor_tensor(WT_l[:, a, :, :], src, WT_h[:, a, :, :].bitcast(F32),
                                          ALU.subtract).then_inc(t_freed, 1)
                elif kind == "xstat":
                    dve.wait_ge(x_in[a // GROUP], 16)
                    row_stats(st, X[:, a, :], a)
                elif kind == "turn_x":
                    n = t_use[st]
                    dve.wait_ge(t_high, n + 1)
                    dve.tensor_tensor(XT_l[:, a % 2, b, :], T_B[n % T_BANKS][:, :],
                                      XT_h[:, a % 2, b, :].bitcast(F32), ALU.subtract).then_inc(t_freed, 1)
                elif kind == "turn_p":
                    n, k, w = t_use[st], p_use[(a, b)] % PT_SLOTS, P * blocks_of(a, b)
                    dve.wait_ge(t_high, n + 1)
                    dve.tensor_tensor(PT_l[:, k, 0:w], T_B[n % T_BANKS][:, 0:w],
                                      PT_h[:, k, 0:w].bitcast(F32), ALU.subtract).then_inc(t_freed, 1)
                elif kind == "proj":
                    n = s_use[st]
                    src = S_B[n % S_BANKS][:, :]
                    dve.wait_ge(s_high, high_no[st] + 1)
                    if b < 4:
                        dve.wait_ge(cols_in, 48)
                        part = (q_part, k_part)[b // 2]
                        dve.scalar_tensor_tensor(part(1, a)[:, b % 2, :], src, cols[:, b // 2, b % 2:b % 2 + 1],
                                                 part(0, a)[:, b % 2, :].bitcast(F32), ALU.add,
                                                 ALU.subtract).then_inc(s_freed, 1)
                    else:
                        t = GROUP * a + 2 * (b - 4)
                        dve.tensor_tensor(V[:, t:t + 2, 1, :], src.rearrange("p (t d) -> p t d", t=2),
                                          V[:, t:t + 2, 0, :].bitcast(F32), ALU.subtract).then_inc(s_freed, 1)
                elif kind == "score":
                    n, w = s_use[st], P * blocks_of(a, b)
                    dve.wait_ge(s_filled, n + 1)
                    if a < 2:
                        dve.wait_ge(t_filled, t_use[("turn_w", 3, 0)] + 1)
                    if a >= 2:
                        dve.wait_ge(t_filled, t_use[("turn_p", a - 2, chunks_of(a - 2) - 1)] + 1)
                    dve.tensor_scalar(SC[:, a % 2, b * 512:b * 512 + w], S_B[n % S_BANKS][:, 0:w], -SCALE, None,
                                      ALU.mult, ALU.min, accum_out=cmin[:, a % 2, b:b + 1]).then_inc(s_freed, 1)
                elif kind == "least":
                    n = chunks_of(a)
                    dve.wait_ge(s_freed, s_use[("score", a, n - 1)] + 1)
                    if a >= 2:
                        dve.wait_ge(probs_ready, e_use[(a - 2, chunks_of(a - 2) - 1)] + 1)
                    dve.tensor_reduce(nmax[:, a % 2:a % 2 + 1], cmin[:, a % 2, 0:n], AX.X, ALU.min).then_inc(min_ready, 1)
                elif kind == "attn_out":
                    dve.wait_ge(pv_done, p_use[(a, chunks_of(a) - 1)] + 1)
                    dve.wait_ge(rl_ready, a + 1)
                    dve.wait_ge(xb_ready, a + 1)
                    dve.scalar_tensor_tensor(X[:, a, :], O_B[:, 0:D], rl[:, a % 2:a % 2 + 1], X[:, a, :],
                                             ALU.mult, ALU.add).then_inc(x1_ready, 1)
                    dve.wait_ge(x1_ready, a + 1)
                    row_stats(st, X[:, a, :], norm_cols(st).start)
                elif kind == "y":
                    dve.wait_ge(rs_ready, norm_no[("attn_out", a, 0)] + 1)
                    if a == 0:
                        dve.wait_ge(table_stored, 32)
                    if a >= 2:
                        dve.wait_ge(yt_filled, a - 1)
                    normed(Y[:, a % 2, :], X[:, a, :], ("attn_out", a, 0), 0, y_ready)
                elif kind == "turn_y":
                    dve.wait_ge(yt_high, a + 1)
                    dve.tensor_tensor(YT_l[:, :, :], Y_B[:, 0:D].rearrange("p (c r) -> p c r", c=DC),
                                      YT_h[:, :, :].bitcast(F32), ALU.subtract).then_inc(yt_low, 1)
                    if a >= TILES - TAIL:
                        add_patches(dve, a)
                elif kind == "x2":
                    dve.wait_ge(h_done, a + 1)
                    dve.wait_ge(patches_added, a + 1)
                    dve.tensor_tensor(X[:, a, :], Y_B[:, 0:D], X[:, a, :], ALU.add).then_inc(x2_ready, 1)
                    dve.wait_ge(x2_ready, a + 1)
                    row_stats(st, X[:, a, :], norm_cols(st).start)
                elif kind == "z":
                    s = a % 2
                    dve.wait_ge(rs_ready, norm_no[("x2", a, 0)] + 1)
                    normed(Z[:, s, :], X[:, a, :], ("x2", a, 0), 0, z_ready)
                    dve.wait_ge(z_ready, a + 1)
                    dve.tensor_reduce(zmax[:, s:s + 1], Z[:, s, :], AX.X, ALU.max,
                                      apply_absolute_value=True).then_inc(z_ready_max, 1)
                elif kind == "bits":
                    s = a % 2
                    if a >= 2:
                        dve.wait_ge(q_ready, a - 1)
                    dve.wait_ge(v_ready, a + 1)
                    dve.tensor_scalar(MG[:, s, :].bitcast(I32), VV[:, s, :].bitcast(I32), 0x7F800000, None,
                                      ALU.bitwise_and).then_inc(bits_ready, 1)
                    dve.wait_ge(z_ready_max, a + 1)
                    dve.tensor_scalar(zmax[:, s:s + 1], zmax[:, s:s + 1], scl[:, 2:3], None,
                                      ALU.mult).then_inc(z_scaled, 1)
                    dve.wait_ge(bits_ready, a + 1)
                    dve.tensor_scalar(MG[:, s, :], MG[:, s, :], 2.0 ** -6, 1.5 * 2.0 ** 20,
                                      ALU.max, ALU.mult).then_inc(magic_ready, 1)
                    if a >= 2:
                        dve.wait_ge(f_ready, a - 1)
                    dve.wait_ge(z_scaled, a + 1)
                    dve.tensor_scalar(nanf[:, s, 0:1], zmax[:, s:s + 1], E4M3_MAX, 3.0e38, ALU.is_gt,
                                      ALU.mult).then_inc(nan_step, 1)
                    dve.wait_ge(nan_step, 2 * a + 1)
                    dve.tensor_scalar(nanf[:, s, 1:2], nanf[:, s, 0:1], 1.0e10, 0.0, ALU.mult,
                                      ALU.mult).then_inc(nan_step, 1)
                    if a >= TILES - TAIL:
                        round_rows(dve, a)
                elif kind == "store" and a >= TILES - TAIL:
                    finish_rows(dve, a)
                elif kind == "quant_k" and b == 0:
                    dve.wait_ge(scl_in, 32)
                    dve.reciprocal(scl[:, 2:4], scl[:, 0:2]).then_inc(scl_ready, 1)
                    dve.tensor_tensor(ss[:, :], scl[:, 0:1], scl[:, 1:2], ALU.mult).then_inc(scl_ready, 1)
                    dve.wait_ge(kern_in, 16)
                    dve.wait_ge(scl_ready, 2)
                    dve.wait_ge(t_filled, t_use[("turn_w", 3, 0)] + 1)
                    dve.tensor_scalar(kv[:, :, :], kraw[:, :, :], scl[:, 3:4], None, ALU.mult).then_inc(kq_step, 1)
                    dve.wait_ge(kq_step, 1)
                    dve.tensor_scalar(km[:, :, :].bitcast(I32), kv[:, :, :].bitcast(I32), 0x7F800000, None,
                                      ALU.bitwise_and).then_inc(kq_step, 1)
                    dve.wait_ge(kq_step, 2)
                    dve.tensor_scalar(km[:, :, :], km[:, :, :], 2.0 ** -6, 1.5 * 2.0 ** 20, ALU.max,
                                      ALU.mult).then_inc(kq_step, 1)
                elif kind == "quant_k":
                    dve.wait_ge(kq_pool, 2)
                    dve.tensor_scalar(km[:, :, :], kv[:, :, :], 3.4028e38 / E4M3_MAX, None,
                                      ALU.mult).then_inc(kq_step, 1)
                    dve.wait_ge(kq_step, 4)
                    dve.tensor_tensor(km[:, :, :], km[:, :, :], km[:, :, :], ALU.subtract).then_inc(kq_step, 1)
                    dve.wait_ge(kq_step, 5)
                    dve.tensor_tensor(kq[:, :, :], kv[:, :, :], km[:, :, :], ALU.add).then_inc(kq_ready, 1)
                elif kind == "ends_limb":
                    dve.wait_ge(lens_in, 32)
                    dve.tensor_scalar(limb[:, 0, :], ln[:, :], 2047, None, ALU.bitwise_and).then_inc(limbs_cut, 1)
                    dve.tensor_scalar(limb[:, 1, :], ln[:, :], 11, 2047, ALU.logical_shift_right,
                                      ALU.bitwise_and).then_inc(limbs_cut, 1)
                    dve.tensor_scalar(limb[:, 2, :], ln[:, :], 22, 1023, ALU.logical_shift_right,
                                      ALU.bitwise_and).then_inc(limbs_cut, 1)
                    dve.wait_ge(limbs_cut, 3)
                    dve.tensor_copy(limf[:, :, :], limb[:, :, :]).then_inc(limbs_float, 1)
                    dve.wait_ge(limbs_float, 1)
                    dve.wait_ge(const_ready, 3)
                    for m in range(3):
                        dve.tensor_tensor_scan(limc[:, m, :], onef[:, 0:PER], limf[:, m, :], 0.0, ALU.mult,
                                               ALU.add).then_inc(limbs_run, 1)
                elif kind == "ends_sum":
                    dve.wait_ge(ends_pe, 1)
                    dve.tensor_copy(limp[:, :], Q_B[:, 0:3]).then_inc(limbs_before, 1)
                elif kind == "ends_int":
                    dve.wait_ge(limbs_run, 3)
                    dve.wait_ge(limbs_before, 1)
                    for m in range(3):
                        dve.tensor_scalar(limt[:, m, :], limc[:, m, :], limp[:, m:m + 1], -1.0 if m == 0 else 0.0,
                                          ALU.add, ALU.add).then_inc(limbs_whole, 1)
                    dve.wait_ge(limbs_whole, 3)
                    for m in range(1, 3):
                        dve.tensor_scalar(limt[:, m, :], limt[:, m, :], 11 * m, None,
                                          ALU.logical_shift_left).then_inc(limbs_shifted, 1)
                elif kind == "ends_place":
                    dve.wait_ge(ends_pool, 2)
                    dve.tensor_scalar(endi[:, 1, :], endi[:, 0, :], P - 1, None, ALU.bitwise_and).then_inc(ends_split, 1)
                    dve.tensor_scalar(endi[:, 2, :], endi[:, 0, :], int(math.log2(P)), TILES - 1,
                                      ALU.logical_shift_right, ALU.bitwise_and).then_inc(ends_split, 1)
                    dve.wait_ge(ends_split, 2)
                    dve.tensor_copy(endf[:, 0:3, :], endi[:, 0:3, :]).then_inc(ends_float, 1)
                    dve.wait_ge(ends_float, 1)
                    dve.tensor_scalar(endf[:, 3, :], endf[:, 0, :], float(S - 1), 100.0, ALU.is_gt,
                                      ALU.mult).then_inc(ends_outside, 1)
                    dve.tensor_scalar(endf[:, 0, :], endf[:, 0, :], float(-S), 100.0, ALU.is_lt,
                                      ALU.mult).then_inc(ends_outside, 1)
                    dve.wait_ge(ends_outside, 2)
                    dve.tensor_tensor(endf[:, 2, :], endf[:, 2, :], endf[:, 3, :], ALU.add).then_inc(ends_kept, 1)
                    dve.wait_ge(ends_kept, 1)
                    dve.tensor_tensor(endf[:, 2, :], endf[:, 2, :], endf[:, 0, :], ALU.add).then_inc(ends_kept, 1)
                elif kind == "ends_hot":
                    dve.wait_ge(const_ready, 10)
                    ks = slice(0, PER // 2) if b == 0 else slice(PER // 2, PER)
                    n = ks.stop - ks.start
                    dve.tensor_tensor(hot_lo[:, ks, :], iota[:, None, :].to_broadcast((P, n, P)),
                                      endf[:, 1, ks, None].to_broadcast((P, n, P)), ALU.is_equal).then_inc(hot_ready, 1)
                    if b == 1:
                        dve.wait_ge(ends_kept, 2)
                        dve.tensor_tensor(hot_hi[:, :, :], iota[:, None, 0:TILES].to_broadcast((P, PER, TILES)),
                                          endf[:, 2, :, None].to_broadcast((P, PER, TILES)),
                                          ALU.is_equal).then_inc(hot_ready, 1)
                elif kind == "ends_mask":
                    dve.wait_ge(ends_pe, 2)
                    dve.tensor_scalar(bmask[:, :], Q_B[:, 0:TILES], 1.0, None, ALU.min).then_inc(bmask_ready, 1)
                elif kind == "ends_rank":
                    dve.wait_ge(ends_pe, 3)
                    dve.tensor_copy(btot[:, 0:2, :], Q_B[:, 0:2 * TILES].rearrange("p (a t) -> p a t", a=2)).then_inc(btot_ready, 1)
                elif kind == "ends_index":
                    dve.wait_ge(btot_ready, 1)
                    dve.tensor_tensor_scan(btot[:, 2, :], onef[:, 0:TILES], btot[:, 1, :], 0.0, ALU.mult,
                                           ALU.add).then_inc(brun_ready, 1)
                    dve.tensor_tensor(btot[:, 3, :], btot[:, 0, :], btot[:, 1, :], ALU.subtract).then_inc(brun_ready, 1)
                    dve.wait_ge(brun_ready, 2)
                    dve.scalar_tensor_tensor(btot[:, 0, :], btot[:, 2, :], -1.0, btot[:, 3, :], ALU.add,
                                             ALU.add).then_inc(rank_ready, 1)
                    dve.wait_ge(rank_ready, 1)
                    dve.tensor_scalar(plug[:, :], btot[:, 0, :], 0.0, float(NPATCH - 1), ALU.max,
                                      ALU.min).then_inc(plug_ready, 1)
                elif kind == "run" and b >= 1:
                    dve.wait_ge(patch_u, b + 1)
                    if b >= 2:
                        dve.wait_ge(patch_run, b - 1)
                    dve.scalar_tensor_tensor(CT[0:PP, b, 0:D], CT[0:PP, b - 1, 0:D], PATCH_A, CT[0:PP, b, 0:D],
                                             ALU.mult, ALU.add).then_inc(patch_run, 1)
                elif kind == "fix":
                    dve.wait_ge(carry_ready, 1)
                    dve.wait_ge(patch_run, PER - 1)
                    dve.scalar_tensor_tensor(CT[0:PP, b, 0:D], carry[0:PP, :], PATCH_A ** (b + 1),
                                             CT[0:PP, b, 0:D], ALU.mult, ALU.add).then_inc(patch_fixed, 1)
                elif kind == "pv" and b == chunks_of(a) - 1:
                    dve.wait_ge(probs_ready, e_use[(a, b)] + 1)
                    dve.tensor_reduce(lall[:, a % 2:a % 2 + 1], lsum[:, a % 2, 0:b + 1], AX.X, ALU.add).then_inc(lall_ready, 1)
                    dve.wait_ge(lall_ready, a + 1)
                    dve.reciprocal(rl[:, a % 2:a % 2 + 1], lall[:, a % 2:a % 2 + 1]).then_inc(rl_ready, 1)


_INS = ["x", "ctx_2048", "mask_BxS2_if0", "L0_attn_Wq", "L0_attn_bq", "L0_attn_Wk", "L0_attn_bk",
        "L0_attn_Wv", "L0_attn_bv", "L0_xattn_W_in", "L0_xattn_b_in", "L0_xattn_g_res", "L0_xattn_g_init",
        "L0_ffn_kernel", "L0_ffn_input_scale", "L0_ffn_kernel_scale", "L0_ffn_bias"]


def kernel(**inputs):
    import numpy as _np
    import concourse.bacc as _bacc
    from concourse import mybir as _mybir
    from concourse.bass_utils import run_bass_kernel_spmd as _run

    nc = _bacc.Bacc("TRN2", target_bir_lowering=False, num_devices=1)
    arrays, args = {}, []
    for name in _INS:
        a = _np.ascontiguousarray(inputs[name])
        arrays[f"in_{name}_dram"] = a
        args.append(nc.dram_tensor(f"in_{name}_dram", a.shape, _mybir.dt.from_np(a.dtype), kind="ExternalInput").ap())
    patches = inputs["ctx_2048"].shape[1]
    rows = inputs["x"].shape
    args.append(nc.dram_tensor("patch_table", (patches, rows[2]), F32, kind="Internal").ap())
    args.append(nc.dram_tensor("out_0_dram", rows, F32, kind="ExternalOutput").ap())
    decoder_layer(nc, *args)
    r = _run(nc, [arrays], core_ids=[0])
    return r.results[0]["out_0_dram"]
```

```python
from contextlib import ExitStack
import math

import concourse.bass as bass
from concourse import mybir

F32 = mybir.dt.float32
F32R = mybir.dt.float32r
BF16 = mybir.dt.bfloat16
I32 = mybir.dt.int32
ALU = mybir.AluOpType
ACT = mybir.ActivationFunctionType
AX = mybir.AxisListType

P = 128
LN_EPS = 1e-5
RMS_EPS = 1e-5
PATCH_EPS = 0.001
PATCH_B = math.exp(-PATCH_EPS)
PATCH_A = -math.expm1(-PATCH_EPS)
E4M3_MAX = 464.0
MASKED = -3.0e38
GROUP = 4
S_BANKS = 3
T_BANKS = 2
TURNS = [10, 10, 10, 13, 7, 8, 14, 8, 10, 10, 10, 10, 10, 10, 10, 16]
AT = {"score": (0, 0, 0, 2.7), "exp": (10.1, 10.2, 10.4, 14.0), "turn_p": (11.8, 12.8, 13.8, 15.8),
      "pv": (15.2, 17, 17.5, 18.0), "attn_out": 18.8, "y": 21.5, "turn_y": 22.8, "h": 25.3, "x2": 25.2,
      "z": 28.0, "bits": 28.7, "turn_q": 34.8, "ffn": 36.3, "store": 37.8, "gather": 7.9, "top": 4.6}
AT_FIRST = {"score": (0,), "top": 1.1, "exp": (6.2,), "turn_p": (11.2,), "pv": (16.1,),
      "attn_out": 18.3}
BEHIND = [61, 56, 51, 46, 38, 36, 33, 24, 21, 16, 11, 6, 1, 0, 0, 0]
FILLERS = [2, 6, 4, 2, 2, 1, 1]
FILL_FROM = 5.0
SIDE = {"square": (6, 14.7), "weigh": (17, 29), "run": (18, 31.5), "fix": (36.5, 48),
      "quant": (1.5, 12), "sum": (13.8, 22.8), "count": (24.3, 34)}
TAIL = 1
PT_SLOTS = 3


def chunks_of(i):
    return i // GROUP + 1


def blocks_of(i, j):
    return min(GROUP, i + 1 - GROUP * j)


def make_plan(tiles, per):
    groups = tiles // GROUP
    plan = [("xstat", u, 0) for u in range(GROUP)] + [("xroot", 0, 0), ("split_w", 0, 0), ("split_w", 1, 0), ("bqk", 0, 0)]
    plan += [("fold_b", 0, 0)] + [("xn", u, 0) for u in range(GROUP)] + [("fold_w", 0, 0)]
    plan += [("turn_x", 0, 0), ("turn_x", 0, 1), ("fold_b", 1, 0), ("keep_b", 0, 0), ("turn_w", 2, 0), ("proj", 0, 0)]
    plan += [("xstat", GROUP + u, 0) for u in range(2)] + [("proj", 0, 1)]
    plan += [("xstat", GROUP + u, 0) for u in range(2, 4)] + [("xroot", 1, 0), ("turn_w", 3, 0)]
    plan += [("proj", 0, m) for m in range(2, 6)] + [("xn", GROUP + u, 0) for u in range(GROUP)]

    slots = {}

    def put(slot, step):
        slots.setdefault(slot, []).append(step)

    begins = [sum(TURNS[:t]) for t in range(tiles)]
    for t in range(tiles):
        at = AT_FIRST if t < GROUP else AT
        for j in range(chunks_of(t)):
            for kind in ("score", "exp", "turn_p", "pv"):
                put(begins[t] + at[kind][j], (kind, t, j))
        put(begins[t] + at["top"], ("top", t, 0))
        put(begins[t] + at["attn_out"], ("attn_out", t, 0))
    for b in range(tiles):
        begin = begins[b] + BEHIND[b]
        for kind in ("gather", "y", "turn_y", "h", "x2", "z", "bits", "turn_q", "ffn", "store"):
            put(begin + AT[kind], (kind, b, 0))
    fill = []
    for g in range(1, groups):
        more = g + 1 < groups
        nxt = range(GROUP * (g + 1), GROUP * (g + 2))
        fill += [[("turn_x", g, 0)], [("turn_x", g, 1)]]
        for m in (0, 1, 2, 4):
            fill.append([("proj", g, m)] + ([("proj", g, m + 1)] if m >= 2 else []))
            if more:
                fill[-1] += {0: [("xstat", t, 0) for t in nxt], 1: [("xroot", g + 1, 0)],
                             2: [("xn", t, 0) for t in nxt[:2]], 4: [("xn", t, 0) for t in nxt[2:]]}[m]
    at = 0
    for turn, count in enumerate(FILLERS):
        for k in range(count):
            for step in fill[at]:
                put(begins[turn] + FILL_FROM + k * (TURNS[turn] - FILL_FROM) / count, step)
            at += 1
    assert at == len(fill)
    for name, side in (
            ("square", [("square", 0, k) for k in range(per)] + [("patch_rms", 0, 0)]),
            ("weigh", [("weigh", 0, k) for k in range(per)]),
            ("run", [("run", 0, k) for k in range(per)] + [("seam", 0, 0)]),
            ("fix", [("fix", 0, k) for k in range(per)]),
            ("quant", [("quant_k", 0, 0), ("quant_k", 0, 1)]),
            ("sum", [("ends_limb", 0, 0), ("ends_sum", 0, 0), ("ends_int", 0, 0), ("ends_add", 0, 0),
                     ("ends_place", 0, 0)]),
            ("count", [("ends_hot", 0, 0), ("ends_hot", 0, 1), ("ends_count", 0, 0), ("ends_mask", 0, 0),
                       ("ends_rank", 0, 0), ("ends_index", 0, 0)])):
        first, last = SIDE[name]
        for n, step in enumerate(side):
            put(first + n * (last - first) / len(side), step)
    for k in sorted(slots):
        plan += slots[k]
    return plan


def decoder_layer(nc, x, ctx_in, lens, Wq, bq, Wk, bk, Wv, bv, W_in, b_in, g_res, g_init,
                  ffn_w, s_in, s_k, ffn_b, table, out):
    _, S, D = x.shape
    _, NPATCH, DG = ctx_in.shape
    TILES = S // P
    DC = D // P
    PER = -(-NPATCH // P)
    FULL = NPATCH // PER
    REST = NPATCH - FULL * PER
    PP = FULL + 1
    SCALE = 1.0 / math.sqrt(D)
    assert D == 256 and S % (P * GROUP) == 0 and 0 < REST < PER and DG == 2 * D
    PLAN = make_plan(TILES, PER)

    s_use = {st: n for n, st in enumerate(st for st in PLAN if st[0] in ("proj", "score"))}
    t_use = {st: n for n, st in enumerate(st for st in PLAN
                                         if st[0] in ("fold_w", "turn_w", "turn_x", "turn_p"))}
    p_use = {st[1:]: n for n, st in enumerate(st for st in PLAN if st[0] == "turn_p")}
    e_use = {st[1:]: n for n, st in enumerate(st for st in PLAN if st[0] == "exp")}
    norm_no = {st: n for n, st in enumerate(st for st in PLAN if st[0] in ("xroot", "attn_out", "x2"))}
    high_no = {st: n for n, st in enumerate(st for st in PLAN if st[0] == "proj")}
    assert [st[1] for st in PLAN if st[0] == "h"] == list(range(TILES))

    x_t = x.rearrange("a (t p) d -> p (a t) d", p=P)
    out_t = out.rearrange("a (t p) d -> p (a t) d", p=P)
    ctx_rows = ctx_in.rearrange("a r d -> (a r) d")

    ctx = ExitStack()
    with ctx:
        def sb(name, shape, dt=F32):
            return ctx.enter_context(nc.sbuf_tensor(name, shape, dt))

        def bank(name):
            return ctx.enter_context(nc.psum_tensor(name, [P, 512], F32))

        def sem(name):
            return ctx.enter_context(nc.semaphore(name))

        X = sb("X", [P, TILES, D])
        XN = sb("XN", [P, GROUP, D])
        XT_h = sb("XT_h", [P, DC, S], F32R)
        XT_l = sb("XT_l", [P, DC, S], F32R)
        GT_h = sb("GT_h", [P, DC, S], F32R)
        GT_l = sb("GT_l", [P, DC, S], F32R)
        V = sb("V", [P, TILES, 2, D], F32R)
        SC = sb("SC", [P, 2, S])
        PT_h = sb("PT_h", [P, PT_SLOTS, GROUP * P], F32R)
        PT_l = sb("PT_l", [P, PT_SLOTS, GROUP * P], F32R)
        Wraw = [SC[:, 0, 512 * m:512 * m + 512].rearrange("p (b d) -> p b d", b=2) for m in range(4)]
        WT_h = sb("WT_h", [P, 3, DC, D], F32R)
        WT_l = sb("WT_l", [P, 3, DC, D], F32R)
        WV_h = sb("WV_h", [P, DC, D + 2], F32R)
        WV_l = sb("WV_l", [P, DC, D + 2], F32R)
        fold = sb("fold", [P, 3, DC])
        bqk = sb("bqk", [P, DC])
        row_term = sb("row_term", [P, TILES])
        CT = sb("CT", [P, PER, DG])
        GB = CT[:, 0:TILES // 2, :].rearrange("p k (h d) -> p (k h) d", h=2)
        late = CT[:, TILES // 2:PER, :].rearrange("p k d -> p (k d)")
        Y, VV, MG = (late[:, 512 * n:512 * (n + 1)].rearrange("p (s d) -> p s d", s=2) for n in range(3))
        Z, Q8, F1 = (late[:, 1536 + 256 * n:1792 + 256 * n].bitcast(BF16).rearrange("p (s d) -> p s d", s=2)
                     for n in range(3))
        carry = SC[:, 0, 1024:1024 + D]
        bv_b = sb("bv_b", [P, D])
        bin_b = sb("bin_b", [P, D])
        ginit_b = sb("ginit_b", [P, D])
        fb_b = sb("fb_b", [P, D], BF16)
        cols = sb("cols", [P, 3, DC])
        scl = sb("scl", [P, 4])
        ss = sb("ss", [P, 1])
        identf = sb("identf", [P, P])
        identb = sb("identb", [P, P], BF16)
        maskb = sb("maskb", [P, P], BF16)
        allf = SC[:, 1, S - 2 * P:S - P]
        tri = SC[:, 1, S - P:S]
        trib = sb("trib", [P, P], BF16)
        onesb = sb("onesb", [P, P], BF16)
        seam = sb("seam", [P, P])
        neg_half = sb("neg_half", [P, 16])
        stats = sb("stats", [P, 2, 6])
        mv = sb("mv", [P, 3 * TILES, 2])
        rs = sb("rs", [P, 3 * TILES])
        negm = sb("negm", [P, GROUP])
        shift = sb("shift", [P, GROUP])
        ve = sb("ve", [P, 3 * TILES])
        cmax = sb("cmax", [P, 2, GROUP])
        top = sb("top", [P, 2])
        nmax = sb("nmax", [P, 2])
        lsum = sb("lsum", [P, 2, GROUP])
        lall = sb("lall", [P, 2])
        rl = sb("rl", [P, 2])
        YT_h = sb("YT_h", [P, DC, P], F32R)
        YT_l = sb("YT_l", [P, DC, P], F32R)
        zmax = sb("zmax", [P, 2])
        nanf = sb("nanf", [P, 2, 2])
        QT8 = sb("QT8", [P, DC, P], BF16)
        kraw = sb("kraw", [P, DC, D], BF16)
        kv, km = (SC[:, 0, 1024 + 512 * n:1536 + 512 * n].rearrange("p (c e) -> p c e", c=DC) for n in range(2))
        kq = sb("kq", [P, DC, D], BF16)
        ln = sb("ln", [P, PER], I32)
        limb = sb("limb", [P, 3, PER], I32)
        limf = sb("limf", [P, 3, PER])
        limc = sb("limc", [P, 3, PER])
        limp = sb("limp", [P, 3])
        limt = sb("limt", [P, 3, PER], I32)
        endi = sb("endi", [P, 4, PER], I32)
        endf = sb("endf", [P, 4, PER])
        iota = sb("iota", [P, P], BF16)
        hot_lo = SC[:, 1, S // 2:S // 2 + PER * P // 2].bitcast(BF16).rearrange("p (k r) -> p k r", r=P)
        hot_hi = sb("hot_hi", [P, PER, TILES], BF16)
        onef = sb("onef", [P, 16])
        bmask = sb("bmask", [P, TILES], BF16)
        btot = sb("btot", [P, 4, TILES])
        plug = sb("plug", [P, TILES], I32)
        ssq = sb("ssq", [P, PER])
        prs = sb("prs", [P, PER])

        S_B = [bank(f"S_B{n}") for n in range(S_BANKS)]
        T_B = [bank(f"T_B{n}") for n in range(T_BANKS)]
        O_B = bank("O_B")
        Y_B = bank("Y_B")
        Q_B = bank("Q_B")

        split_high = sem("split_high")
        split_low = sem("split_low")
        bqk_ready = sem("bqk_ready")
        fold_done = sem("fold_done")
        fold_kept = sem("fold_kept")
        qk_high = sem("qk_high")
        qk_low = sem("qk_low")
        top_ready = sem("top_ready")
        allf_ready = sem("allf_ready")
        x_in = [sem(f"x_in{g}") for g in range(TILES // GROUP)]
        w_in = [sem(f"w_in{m}") for m in range(4)]
        biases_in = sem("biases_in")
        gres_in = sem("gres_in")
        bin_in = sem("bin_in")
        rows_in = sem("rows_in")
        bv_in = sem("bv_in")
        scl_in = sem("scl_in")
        kern_in = sem("kern_in")
        lens_in = sem("lens_in")
        ctx_loaded = sem("ctx_loaded")
        const_ready = sem("const_ready")
        const_step = sem("const_step")
        scl_ready = sem("scl_ready")
        stats_ready = sem("stats_ready")
        mv_ready = sem("mv_ready")
        ve_ready = sem("ve_ready")
        rs_ready = sem("rs_ready")
        xn_ready = sem("xn_ready")
        negm_ready = sem("negm_ready")
        shift_ready = sem("shift_ready")
        xb_ready = sem("xb_ready")
        s_filled = sem("s_filled")
        s_high = sem("s_high")
        s_freed = sem("s_freed")
        t_filled = sem("t_filled")
        t_high = sem("t_high")
        t_freed = sem("t_freed")
        nmax_ready = sem("nmax_ready")
        probs_ready = sem("probs_ready")
        rl_ready = sem("rl_ready")
        lall_ready = sem("lall_ready")
        pv_done = sem("pv_done")
        x1_ready = sem("x1_ready")
        y_ready = sem("y_ready")
        patches_added = sem("patches_added")
        yt_filled = sem("yt_filled")
        yt_high = sem("yt_high")
        yt_low = sem("yt_low")
        h_done = sem("h_done")
        x2_ready = sem("x2_ready")
        z_ready = sem("z_ready")
        v_ready = sem("v_ready")
        z_ready_max = sem("z_ready_max")
        z_scaled = sem("z_scaled")
        bits_ready = sem("bits_ready")
        magic_ready = sem("magic_ready")
        nan_step = sem("nan_step")
        round_step = sem("round_step")
        q_ready = sem("q_ready")
        qt_filled = sem("qt_filled")
        qt_ready = sem("qt_ready")
        ffn_done = sem("ffn_done")
        f_ready = sem("f_ready")
        f_step = sem("f_step")
        out_ready = sem("out_ready")
        out_stored = sem("out_stored")
        kq_step = sem("kq_step")
        kq_pool = sem("kq_pool")
        kq_ready = sem("kq_ready")
        ends_pool = sem("ends_pool")
        ends_pe = sem("ends_pe")
        patch_sq = sem("patch_sq")
        patch_rs = sem("patch_rs")
        patch_u = sem("patch_u")
        patch_run = sem("patch_run")
        patch_fixed = sem("patch_fixed")
        patch_gained = sem("patch_gained")
        patch_whole = sem("patch_whole")
        gain_in = sem("gain_in")
        patch_pe = sem("patch_pe")
        carry_ready = sem("carry_ready")
        table_stored = sem("table_stored")
        gathered = [sem(f"gathered{t}") for t in range(TILES)]
        limbs_cut = sem("limbs_cut")
        limbs_float = sem("limbs_float")
        limbs_run = sem("limbs_run")
        limbs_before = sem("limbs_before")
        limbs_whole = sem("limbs_whole")
        limbs_shifted = sem("limbs_shifted")
        ends_split = sem("ends_split")
        ends_float = sem("ends_float")
        ends_outside = sem("ends_outside")
        ends_kept = sem("ends_kept")
        hot_ready = sem("hot_ready")
        bmask_ready = sem("bmask_ready")
        btot_ready = sem("btot_ready")
        brun_ready = sem("brun_ready")
        rank_ready = sem("rank_ready")
        plug_ready = sem("plug_ready")

        def g_part(part, g):
            return (GT_h, GT_l)[part][:, :, g * GROUP * P:(g + 1) * GROUP * P]

        def x_part(part, g):
            return (XT_h, XT_l)[part][:, :, g * GROUP * P:(g + 1) * GROUP * P]

        block = ctx.enter_context(nc.Block())

        def norm_cols(st):
            kind, a, _ = st
            first = {"xroot": GROUP * a, "attn_out": TILES + a, "x2": 2 * TILES + a}[kind]
            return slice(first, first + norm_tiles(st))

        def norm_tiles(st):
            return GROUP if st[0] == "xroot" else 1

        stat_no = {st: n for n, st in enumerate(st for st in PLAN if st[0] in ("xstat", "attn_out", "x2"))}

        def stats_of(st):
            return stat_no[("xstat", GROUP * st[1] + GROUP - 1, 0) if st[0] == "xroot" else st] + 1


        @block.sync
        def _(sp):
            def row(dst, src, done):
                sp.dma_start(dst, src.rearrange("(a n) -> a n", a=1).to_broadcast((P, src.shape[0]))).then_inc(done, 16)

            sp.dma_start(X[:, 0:GROUP, :], x_t[:, 0:GROUP, :]).then_inc(x_in[0], 16)
            for m, w in ((1, Wk), (2, Wv)):
                sp.dma_start(Wraw[m], w.rearrange("(b p) d -> p b d", p=P)).then_inc(w_in[m], 16)
            sp.dma_start(X[:, GROUP:2 * GROUP, :], x_t[:, GROUP:2 * GROUP, :]).then_inc(x_in[1], 16)
            sp.dma_start(Wraw[3], W_in.rearrange("(b p) d -> p b d", p=P)).then_inc(w_in[3], 16)
            row(bv_b[:, :], bv, bv_in)
            sp.dma_start(CT[0:FULL, :, :],
                         ctx_rows[0:FULL * PER, :].rearrange("(p k) d -> p k d", k=PER)).then_inc(ctx_loaded, 16)
            sp.dma_start(CT[FULL:PP, 0:REST, :],
                         ctx_rows[FULL * PER:NPATCH, :].rearrange("(p k) d -> p k d", k=REST)).then_inc(ctx_loaded, 16)
            row(ginit_b[:, :], g_init[0:D], gain_in)
            sp.dma_start(CT[FULL:PP, REST:PER, :],
                         ctx_rows[0:PER - REST, :].rearrange("(p k) d -> p k d", k=PER - REST)).then_inc(ctx_loaded, 16)
            for g in range(2, TILES // GROUP):
                sp.dma_start(X[:, g * GROUP:(g + 1) * GROUP, :],
                             x_t[:, g * GROUP:(g + 1) * GROUP, :]).then_inc(x_in[g], 16)
            sp.dma_start(kraw[:, :, :], ffn_w.rearrange("(c p) e -> p c e", p=P)).then_inc(kern_in, 16)
            row(scl[:, 0:1], s_in, scl_in)
            row(scl[:, 1:2], s_k, scl_in)
            row(bin_b[:, :], b_in, bin_in)
            row(fb_b[:, :], ffn_b, rows_in)
            sp.wait_ge(patch_whole, PER)
            sp.dma_start(table[0:FULL * PER, :].rearrange("(p k) d -> p k d", k=PER),
                         CT[0:FULL, :, 0:D]).then_inc(table_stored, 16)
            sp.dma_start(table[FULL * PER:NPATCH, :].rearrange("(p k) d -> p k d", k=REST),
                         CT[FULL:PP, 0:REST, 0:D]).then_inc(table_stored, 16)
            for b in range(TILES):
                sp.wait_ge(out_ready, b + 1)
                sp.dma_start(out_t[:, b, :], X[:, b, :]).then_inc(out_stored, 16)
            sp.wait_ge(out_stored, 16 * TILES)
            sp.wait_ge(table_stored, 32)

        def in_tail(st):
            return st[0] != "xroot" and st[1] >= TILES - TAIL

        def padded_var(eng, st, mul, add):
            s = norm_cols(st)
            eng.wait_ge(mv_ready, stats_of(st))
            eng.tensor_scalar(ve[:, s], mv[:, s, 1], mul, add, ALU.mult, ALU.add).then_inc(ve_ready, 1)

        def add_patches(eng, a):
            eng.wait_ge(gathered[a], 16)
            eng.wait_ge(y_ready, a + 1)
            eng.tensor_tensor(X[:, a, :], X[:, a, :], GB[:, a, :], ALU.add).then_inc(patches_added, 1)

        def round_rows(eng, a):
            s = a % 2
            if a == TILES - TAIL:
                eng.wait_ge(q_ready, a)
            eng.wait_ge(magic_ready, a + 1)
            eng.tensor_tensor(VV[:, s, :], VV[:, s, :], MG[:, s, :], ALU.add).then_inc(round_step, 1)
            eng.wait_ge(round_step, a + 1)
            if a >= 2:
                eng.wait_ge(qt_filled, a - 1)
            eng.tensor_tensor(Q8[:, s, :], VV[:, s, :], MG[:, s, :], ALU.subtract).then_inc(q_ready, 1)

        def finish_rows(eng, a):
            s = a % 2
            if a == TILES - TAIL:
                eng.wait_ge(out_ready, a)
            eng.wait_ge(rows_in, 16)
            eng.wait_ge(f_ready, a + 1)
            eng.tensor_tensor(F1[:, s, :], F1[:, s, :], fb_b[:, :], ALU.add).then_inc(f_step, 1)
            eng.wait_ge(f_step, a + 1)
            eng.tensor_tensor(X[:, a, :], X[:, a, :], F1[:, s, :], ALU.add).then_inc(out_ready, 1)

        @block.gpsimd
        def _(pool):
            pool.memset(identf[:, :], 0.0).then_inc(const_step, 1)
            pool.memset(identb[:, :], 0.0).then_inc(const_step, 1)
            pool.memset(maskb[:, :], 0.0).then_inc(const_step, 1)
            pool.memset(tri[:, :], 0.0).then_inc(const_step, 1)
            pool.memset(trib[:, :], 1.0).then_inc(const_step, 1)
            pool.memset(seam[:, :], 0.0).then_inc(const_step, 1)
            pool.memset(onesb[:, :], 1.0).then_inc(const_ready, 1)
            pool.memset(allf[:, :], 1.0).then_inc(allf_ready, 1)
            pool.memset(neg_half[:, :], -0.5).then_inc(const_ready, 1)
            pool.memset(onef[:, :], 1.0).then_inc(const_ready, 1)
            pool.wait_ge(const_step, 6)
            for m in (identf, identb):
                pool.affine_select(out=m[:, :], in_=m[:, :], compare_op=ALU.not_equal, fill=1.0, base=0,
                                   pattern=[[-1, P]], channel_multiplier=1).then_inc(const_ready, 1)
            pool.affine_select(out=maskb[:, :], in_=maskb[:, :], compare_op=ALU.is_ge, fill=MASKED, base=0,
                               pattern=[[-1, P]], channel_multiplier=1).then_inc(const_ready, 1)
            pool.wait_ge(const_ready, 5)
            pool.memset(ln[:, :], 0).then_inc(const_step, 1)
            pool.affine_select(out=tri[:, :], in_=tri[:, :], compare_op=ALU.is_ge, fill=1.0, base=0,
                               pattern=[[-1, P]], channel_multiplier=1).then_inc(const_ready, 1)
            pool.affine_select(out=trib[:, :], in_=trib[:, :], compare_op=ALU.is_ge, fill=0.0, base=0,
                               pattern=[[1, P]], channel_multiplier=-1).then_inc(const_ready, 1)
            pool.affine_select(out=seam[:, :], in_=seam[:, :], compare_op=ALU.not_equal, fill=1.0, base=1,
                               pattern=[[-1, P]], channel_multiplier=1).then_inc(const_step, 1)
            pool.wait_ge(const_step, 8)
            pool.affine_select(out=seam[:, :], in_=seam[:, :], compare_op=ALU.not_equal,
                               fill=PATCH_A ** PER, base=2,
                               pattern=[[-1, P]], channel_multiplier=1).then_inc(const_ready, 1)
            pool.iota(iota[:, :], pattern=[[1, P]], base=0, channel_multiplier=0,
                      allow_small_or_imprecise_dtypes=True).then_inc(const_ready, 1)
            pool.dma_start(ln[0:FULL, :], lens[0, 0:FULL * PER].rearrange("(p k) -> p k", k=PER)).then_inc(lens_in, 16)
            pool.dma_start(ln[FULL:PP, 0:REST],
                           lens[0, FULL * PER:NPATCH].rearrange("(p k) -> p k", k=REST)).then_inc(lens_in, 16)

            def rsqrt_of_var(st, mul, add):
                s, n, no = norm_cols(st), norm_tiles(st), norm_no[st]
                if not in_tail(st):
                    padded_var(pool, st, mul, add)
                pool.wait_ge(ve_ready, no + 1)
                pool.tensor_tensor(rs[:, s], ve[:, s], neg_half[:, 0:n], ALU.pow).then_inc(rs_ready, 1)

            for st in PLAN:
                kind, a, b = st
                if kind == "xroot":
                    cs = norm_cols(st)
                    rsqrt_of_var(st, 1.0, LN_EPS)
                    pool.tensor_scalar(negm[:, :], mv[:, cs, 0], -1.0, 0.0, ALU.mult, ALU.add).then_inc(negm_ready, 1)
                    pool.wait_ge(rs_ready, norm_no[st] + 1)
                    pool.wait_ge(negm_ready, a + 1)
                    if a >= 1:
                        pool.wait_ge(xn_ready, GROUP * a)
                    pool.tensor_tensor(shift[:, :], negm[:, :], rs[:, cs], ALU.mult).then_inc(shift_ready, 1)
                elif kind == "xn":
                    pool.wait_ge(bv_in, 16)
                    pool.wait_ge(xn_ready, a + 1)
                    pool.tensor_tensor(X[:, a, :], X[:, a, :], bv_b[:, :], ALU.add).then_inc(xb_ready, 1)
                elif kind == "attn_out":
                    rsqrt_of_var(st, 1.0 + RMS_EPS, RMS_EPS * LN_EPS)
                elif kind == "square":
                    pool.wait_ge(gain_in, 16)
                    pool.wait_ge(patch_sq, b + 1)
                    pool.tensor_tensor(CT[0:PP, b, 0:D], CT[0:PP, b, 0:D], ginit_b[0:PP, :],
                                       ALU.mult).then_inc(patch_gained, 1)
                elif kind == "fix":
                    pool.wait_ge(bin_in, 16)
                    pool.wait_ge(patch_fixed, b + 1)
                    pool.tensor_tensor(CT[0:PP, b, 0:D], CT[0:PP, b, 0:D], bin_b[0:PP, :],
                                       ALU.add).then_inc(patch_whole, 1)
                elif kind == "turn_y" and a < TILES - TAIL:
                    add_patches(pool, a)
                elif kind == "x2":
                    rsqrt_of_var(st, 1.0, LN_EPS)
                elif kind == "bits" and a < TILES - TAIL:
                    round_rows(pool, a)
                elif kind == "store" and a < TILES - TAIL:
                    finish_rows(pool, a)
                elif kind == "quant_k" and b == 0:
                    pool.wait_ge(kq_step, 3)
                    pool.tensor_tensor(kv[:, :, :], kv[:, :, :], km[:, :, :], ALU.add).then_inc(kq_pool, 1)
                    pool.wait_ge(kq_pool, 1)
                    pool.tensor_tensor(kv[:, :, :], kv[:, :, :], km[:, :, :], ALU.subtract).then_inc(kq_pool, 1)
                elif kind == "ends_add":
                    pool.wait_ge(limbs_shifted, 2)
                    pool.tensor_tensor(endi[:, 0, :], limt[:, 0, :], limt[:, 1, :], ALU.add).then_inc(ends_pool, 1)
                    pool.wait_ge(ends_pool, 1)
                    pool.tensor_tensor(endi[:, 0, :], endi[:, 0, :], limt[:, 2, :], ALU.add).then_inc(ends_pool, 1)
                elif kind == "patch_rms":
                    pool.wait_ge(patch_sq, PER)
                    pool.tensor_scalar(prs[0:PP, :], ssq[0:PP, :], 1.0 / DG, RMS_EPS, ALU.mult, ALU.add).then_inc(patch_rs, 1)
                    pool.wait_ge(patch_rs, 1)
                    pool.tensor_tensor(prs[0:PP, :], prs[0:PP, :], neg_half[0:PP, 0:PER], ALU.pow).then_inc(patch_rs, 1)
                    pool.wait_ge(patch_rs, 2)
                    pool.tensor_scalar(prs[0:PP, :], prs[0:PP, :], PATCH_B, 0.0, ALU.mult, ALU.add).then_inc(patch_rs, 1)
                elif kind == "gather":
                    pool.wait_ge(table_stored, 32)
                    pool.wait_ge(plug_ready, 1)
                    pool.indirect_dma_start(GB[:, a, :], None, table[:, :],
                                            bass.IndirectOffsetOnAxis(plug[:, a:a + 1].bitcast(mybir.dt.uint32), 0),
                                            bounds_check=NPATCH - 1).then_inc(gathered[a], 16)

        @block.scalar
        def _(act):
            for n, col in enumerate((bq, bk, g_res)):
                if n == 2:
                    act.dma_start(Wraw[0], Wq.rearrange("(b p) d -> p b d", p=P)).then_inc(w_in[0], 16)
                act.dma_start(cols[:, n, :], col.rearrange("(c p) -> p c", p=P),
                              allow_slow_non_contiguous=True).then_inc((biases_in, biases_in, gres_in)[n], 16)

            for st in PLAN:
                kind, a, b = st
                if kind == "split_w":
                    act.wait_ge(w_in[a], 16)
                    act.activation(WT_h[:, (2, 1)[a], :, :], Wraw[a], ACT.Copy).then_inc(split_high, 1)
                elif kind == "keep_b":
                    act.wait_ge(fold_kept, 1)
                    act.activation(WV_h[:, :, D:D + 2], fold[:, 1, :, None].to_broadcast((P, DC, 2)),
                                   ACT.Copy).then_inc(qk_high, 1)
                elif kind in ("turn_w", "fold_w"):
                    n = t_use[st]
                    act.wait_ge(t_filled, n + 1)
                    src = T_B[n % T_BANKS][:, :].rearrange("p (c e) -> p c e", c=DC)
                    if a == 3:
                        act.wait_ge(gres_in, 16)
                        act.activation(WT_h[:, 2, 0, :], src[:, 0, :], ACT.Copy, scale=cols[:, 2, 0:1])
                        act.activation(WT_h[:, 2, 1, :], src[:, 1, :], ACT.Copy,
                                       scale=cols[:, 2, 1:2]).then_inc(t_high, 1)
                    else:
                        dst = WV_h[:, :, 0:D] if a == 2 else WT_h[:, 0, :, :]
                        act.activation(dst, src, ACT.Copy).then_inc(t_high, 1)
                elif kind == "xn":
                    g, u = a // GROUP, a % GROUP
                    act.wait_ge(shift_ready, g + 1)
                    if g >= 1:
                        act.wait_ge(t_filled, t_use[("turn_x", g - 1, 1)] + 1)
                    act.activation(XN[:, u, :], X[:, a, :], ACT.Identity, bias=shift[:, u:u + 1],
                                   scale=rs[:, a:a + 1]).then_inc(xn_ready, 1)
                elif kind == "turn_x":
                    n = t_use[st]
                    act.wait_ge(t_filled, n + 1)
                    act.activation(x_part(0, a)[:, b, :], T_B[n % T_BANKS][:, :], ACT.Copy).then_inc(t_high, 1)
                elif kind == "turn_p":
                    n, k, w = t_use[st], p_use[(a, b)], P * blocks_of(a, b)
                    act.wait_ge(t_filled, n + 1)
                    if k >= PT_SLOTS:
                        act.wait_ge(pv_done, k - PT_SLOTS + 1)
                    act.activation(PT_h[:, k % PT_SLOTS, 0:w], T_B[n % T_BANKS][:, 0:w], ACT.Copy).then_inc(t_high, 1)
                elif kind == "proj":
                    n = s_use[st]
                    act.wait_ge(s_filled, n + 1)
                    src = S_B[n % S_BANKS][:, :]
                    if b < 2:
                        act.wait_ge(fold_kept, 1)
                        act.activation(g_part(0, a)[:, b, :], src, ACT.Identity,
                                       bias=fold[:, 0, b:b + 1]).then_inc(s_high, 1)
                    else:
                        act.activation(V[:, GROUP * a + b - 2, 0, :], src[:, 0:D], ACT.Copy).then_inc(s_high, 1)
                elif kind == "exp":
                    w = P * blocks_of(a, b)
                    act.wait_ge(nmax_ready, a + 1)
                    if a >= 2 and b == 0:
                        act.wait_ge(rl_ready, a - 1)
                    part = SC[:, a % 2, b * 512:b * 512 + w]
                    act.activation(part, part, ACT.Exp, scale=SCALE, bias=nmax[:, a % 2:a % 2 + 1],
                                   accum_out=lsum[:, a % 2, b:b + 1]).then_inc(probs_ready, 1)
                elif kind == "turn_y":
                    act.wait_ge(yt_filled, a + 1)
                    act.activation(YT_h[:, :, :], Y_B[:, 0:D].rearrange("p (c r) -> p c r", c=DC),
                                   ACT.Copy).then_inc(yt_high, 1)
                elif kind == "turn_q":
                    act.wait_ge(qt_filled, a + 1)
                    act.activation(QT8[:, :, :], Q_B[:, 0:P].bitcast(BF16).rearrange("p (c r) -> p c r", c=DC),
                                   ACT.Copy).then_inc(qt_ready, 1)
                elif kind == "ffn":
                    act.wait_ge(ffn_done, a + 1)
                    act.wait_ge(nan_step, 2 * (a + 1))
                    act.wait_ge(scl_ready, 2)
                    if a >= 2:
                        act.wait_ge(out_ready, a - 1)
                    act.activation(F1[:, a % 2, :], Q_B[:, 0:D], ACT.Identity, scale=ss[:, 0:1],
                                   bias=nanf[:, a % 2, 1:2]).then_inc(f_ready, 1)
                elif kind == "square":
                    act.wait_ge(ctx_loaded, 48)
                    if b >= 2:
                        act.wait_ge(patch_sq, b - 1)
                    act.activation((Q_B, Y_B)[b % 2][0:PP, :], CT[0:PP, b, :], ACT.Square,
                                   accum_out=ssq[0:PP, b:b + 1]).then_inc(patch_sq, 1)
                elif kind == "weigh":
                    act.wait_ge(patch_rs, 3)
                    act.wait_ge(patch_gained, b + 1)
                    act.activation(CT[0:PP, b, 0:D], CT[0:PP, b, 0:D], ACT.Copy,
                                   scale=prs[0:PP, b:b + 1]).then_inc(patch_u, 1)
                elif kind == "seam":
                    act.wait_ge(patch_pe, 1)
                    act.activation(carry[0:PP, :], Y_B[0:PP, 0:D], ACT.Copy).then_inc(carry_ready, 1)
                elif kind == "z" and a < TILES - TAIL:
                    act.wait_ge(z_ready, a + 1)
                    act.wait_ge(scl_ready, 2)
                    if a >= 2:
                        act.wait_ge(q_ready, a - 1)
                    act.activation(VV[:, a % 2, :], Z[:, a % 2, :], ACT.Copy, scale=scl[:, 2:3]).then_inc(v_ready, 1)

        @block.tensor
        def _(pe):
            pe.wait_ge(const_ready, 6)

            def three_pass(ps, st_h, st_l, mv_h, mv_l, first, last):
                pe.matmul(ps, st_h, mv_h, start=first, stop=False)
                pe.matmul(ps, st_h, mv_l, start=False, stop=False)
                return pe.matmul(ps, st_l, mv_h, start=False, stop=last)

            def take_s(st):
                n = s_use[st]
                if n >= S_BANKS:
                    pe.wait_ge(s_freed, n - S_BANKS + 1)
                return S_B[n % S_BANKS]

            def take_t(st):
                n = t_use[st]
                if n >= T_BANKS:
                    pe.wait_ge(t_freed, n - T_BANKS + 1)
                return T_B[n % T_BANKS]

            for st in PLAN:
                kind, a, b = st
                if kind == "fold_w":
                    pe.wait_ge(split_low, 2)
                    ps = take_t(st)
                    for c in range(DC):
                        for e in range(DC):
                            mm = three_pass(ps[:, c * D:(c + 1) * D], WT_h[:, 2, e, c * P:(c + 1) * P],
                                            WT_l[:, 2, e, c * P:(c + 1) * P], WT_h[:, 1, e, :], WT_l[:, 1, e, :],
                                            e == 0, e == DC - 1)
                    mm.then_inc(t_filled, 1)
                elif kind == "fold_b":
                    pe.wait_ge(biases_in, 32)
                    pe.wait_ge(w_in[1 - a], 16)
                    for c in range(DC):
                        for e in range(DC):
                            pe.matmul(O_B[:, a * DC + c:a * DC + c + 1], Wraw[1 - a][:, e, c * P:(c + 1) * P],
                                      cols[:, a, e:e + 1], start=(e == 0), stop=(e == DC - 1))
                    if a == 1:
                        pe.wait_ge(bqk_ready, 1)
                        pe.wait_ge(allf_ready, 1)
                        pe.matmul(O_B[:, 2 * DC:3 * DC], allf[:, :], bqk[:, :], start=True, stop=True).then_inc(fold_done, 1)
                elif kind == "turn_w":
                    pe.wait_ge(w_in[a], 16)
                    ps = take_t(st)
                    for c in range(DC):
                        for e in range(DC):
                            mm = pe.transpose(ps[:, c * D + e * P:c * D + (e + 1) * P],
                                              Wraw[a][:, e, c * P:(c + 1) * P], identf[:, :])
                    mm.then_inc(t_filled, 1)
                elif kind == "turn_x":
                    pe.wait_ge(xn_ready, GROUP * (a + 1))
                    ps = take_t(st)
                    for t in range(GROUP):
                        mm = pe.transpose(ps[:, t * P:(t + 1) * P], XN[:, t, b * P:(b + 1) * P], identf[:, :])
                    mm.then_inc(t_filled, 1)
                elif kind == "proj":
                    pe.wait_ge(t_freed, t_use[("turn_x", a, 1)] + 1)
                    pe.wait_ge(t_freed, t_use[("fold_w", 0, 0) if b < 2 else ("turn_w", 2, 0)] + 1)
                    ps, xh, xl = take_s(st), x_part(0, a), x_part(1, a)
                    if b < 2:
                        e = slice(b * P, (b + 1) * P)
                        for c in range(DC):
                            mm = three_pass(ps[:, :], WT_h[:, 0, c, e], WT_l[:, 0, c, e],
                                            xh[:, c, :], xl[:, c, :], c == 0, c == DC - 1)
                    else:
                        pe.wait_ge(qk_low, 1)
                        r = slice((b - 2) * P, (b - 1) * P)
                        for c in range(DC):
                            mm = three_pass(ps[:, 0:D + 2], xh[:, c, r], xl[:, c, r], WV_h[:, c, :], WV_l[:, c, :],
                                            c == 0, c == DC - 1)
                    mm.then_inc(s_filled, 1)
                elif kind == "score":
                    pe.wait_ge(s_freed, s_use[("proj", a // GROUP, 1)] + 1)
                    pe.wait_ge(t_freed, t_use[("turn_x", b, 1)] + 1)
                    ps, n = take_s(st), blocks_of(a, b)
                    g, r = a // GROUP, slice(a % GROUP * P, (a % GROUP + 1) * P)
                    diagonal = b == chunks_of(a) - 1
                    for c in range(DC):
                        mm = three_pass(ps[:, 0:n * P], g_part(0, g)[:, c, r], g_part(1, g)[:, c, r],
                                        x_part(0, b)[:, c, 0:n * P], x_part(1, b)[:, c, 0:n * P],
                                        c == 0, c == DC - 1 and not diagonal)
                    if diagonal:
                        mm = pe.matmul(ps[:, (n - 1) * P:n * P], identb[:, :], maskb[:, :], start=False, stop=True)
                    mm.then_inc(s_filled, 1)
                elif kind == "turn_p":
                    pe.wait_ge(probs_ready, e_use[(a, b)] + 1)
                    ps = take_t(st)
                    for u in range(blocks_of(a, b)):
                        k = (b * GROUP + u) * P
                        mm = pe.transpose(ps[:, u * P:(u + 1) * P], SC[:, a % 2, k:k + P], identf[:, :])
                    mm.then_inc(t_filled, 1)
                elif kind == "pv":
                    pe.wait_ge(t_freed, t_use[("turn_p", a, b)] + 1)
                    if b == 0:
                        if a == 0:
                            pe.wait_ge(fold_kept, 1)
                        if a >= 1:
                            pe.wait_ge(x1_ready, a)
                    slot, n = p_use[(a, b)] % PT_SLOTS, blocks_of(a, b)
                    pe.wait_ge(s_freed, s_use[("proj", b, n + 1)] + 1)
                    for u in range(n):
                        t, r = b * GROUP + u, slice(u * P, (u + 1) * P)
                        mm = three_pass(O_B[:, 0:D], PT_h[:, slot, r], PT_l[:, slot, r], V[:, t, 0, :], V[:, t, 1, :],
                                        t == 0, t == a)
                    mm.then_inc(pv_done, 1)
                elif kind == "turn_y":
                    pe.wait_ge(y_ready, a + 1)
                    if a == 0:
                        pe.wait_ge(carry_ready, 1)
                    if a >= 1:
                        pe.wait_ge(x2_ready, a)
                    for c in range(DC):
                        mm = pe.transpose(Y_B[:, c * P:(c + 1) * P], Y[:, a % 2, c * P:(c + 1) * P], identf[:, :])
                    mm.then_inc(yt_filled, 1)
                elif kind == "h":
                    pe.wait_ge(yt_low, a + 1)
                    pe.wait_ge(t_freed, t_use[("turn_w", 3, 0)] + 1)
                    for c in range(DC):
                        mm = three_pass(Y_B[:, 0:D], YT_h[:, c, :], YT_l[:, c, :], WT_h[:, 2, c, :], WT_l[:, 2, c, :],
                                        c == 0, c == DC - 1)
                    mm.then_inc(h_done, 1)
                elif kind == "turn_q":
                    pe.wait_ge(q_ready, a + 1)
                    if a >= 1:
                        pe.wait_ge(f_ready, a)
                    if a == 0:
                        pe.wait_ge(btot_ready, 1)
                    for c in range(DC):
                        mm = pe.transpose(Q_B[:, 0:P].bitcast(BF16)[:, c * P:(c + 1) * P],
                                          Q8[:, a % 2, c * P:(c + 1) * P], identb[:, :])
                    mm.then_inc(qt_filled, 1)
                elif kind == "ffn":
                    pe.wait_ge(qt_ready, a + 1)
                    pe.wait_ge(kq_ready, 1)
                    for c in range(DC):
                        mm = pe.matmul(Q_B[:, 0:D], QT8[:, c, :], kq[:, c, :], start=(c == 0), stop=(c == DC - 1))
                    mm.then_inc(ffn_done, 1)
                elif kind == "ends_sum":
                    pe.wait_ge(const_ready, 10)
                    pe.wait_ge(patch_sq, PER)
                    pe.wait_ge(limbs_run, 3)
                    pe.matmul(Q_B[:, 0:3], tri[:, :], limc[:, :, PER - 1], start=True, stop=True).then_inc(ends_pe, 1)
                elif kind == "ends_count":
                    pe.wait_ge(hot_ready, 3)
                    pe.wait_ge(limbs_before, 1)
                    for k in range(PER):
                        mm = pe.matmul(Q_B[:, 0:TILES], hot_lo[:, k, :], hot_hi[:, k, :],
                                       start=(k == 0), stop=(k == PER - 1))
                    mm.then_inc(ends_pe, 1)
                elif kind == "ends_rank":
                    pe.wait_ge(bmask_ready, 1)
                    pe.matmul(Q_B[:, 0:TILES], trib[:, :], bmask[:, :], start=True, stop=True)
                    pe.matmul(Q_B[:, TILES:2 * TILES], onesb[:, :], bmask[:, :], start=True, stop=True,
                              skip_group_check=True).then_inc(ends_pe, 1)
                elif kind == "seam":
                    pe.wait_ge(const_ready, 10)
                    pe.wait_ge(patch_run, PER - 1)
                    pe.matmul(Y_B[0:PP, 0:D], seam[0:PP, 0:PP], CT[0:PP, PER - 1, 0:D],
                              start=True, stop=True).then_inc(patch_pe, 1)

        @block.vector
        def _(dve):
            def row_stats(st, row, col):
                no = stat_no[st]
                dve.bn_stats(stats[:, no % 2, :], row).then_inc(stats_ready, 1)
                dve.wait_ge(stats_ready, no + 1)
                dve.bn_aggr(mv[:, col, :], stats[:, no % 2, :]).then_inc(mv_ready, 1)

            def greatest_z(a):
                s = a % 2
                dve.tensor_reduce(zmax[:, s:s + 1], Z[:, s, :], AX.X, ALU.max,
                                  apply_absolute_value=True).then_inc(z_ready_max, 1)

            def scaled_greatest_z(a):
                s = a % 2
                dve.wait_ge(z_ready_max, a + 1)
                dve.tensor_scalar(zmax[:, s:s + 1], zmax[:, s:s + 1], scl[:, 2:3], None,
                                  ALU.mult).then_inc(z_scaled, 1)

            def normed(dst, src, st, u, done):
                s = norm_cols(st).start + u
                dve.tensor_scalar(dst, src, mv[:, s, 0:1], rs[:, s:s + 1],
                                  ALU.subtract, ALU.mult).then_inc(done, 1)

            for st in PLAN:
                kind, a, b = st
                if kind == "split_w":
                    dve.wait_ge(split_high, a + 1)
                    dve.tensor_tensor(WT_l[:, (2, 1)[a], :, :], Wraw[a], WT_h[:, (2, 1)[a], :, :].bitcast(F32),
                                      ALU.subtract).then_inc(split_low, 1)
                elif kind == "bqk":
                    dve.wait_ge(biases_in, 32)
                    dve.tensor_tensor(bqk[:, :], cols[:, 0, :], cols[:, 1, :], ALU.mult).then_inc(bqk_ready, 1)
                elif kind == "keep_b":
                    dve.wait_ge(fold_done, 1)
                    dve.tensor_copy(fold.rearrange("p m c -> p (m c)"), O_B[:, 0:3 * DC]).then_inc(fold_kept, 1)
                    dve.wait_ge(fold_kept, 1)
                    dve.wait_ge(qk_high, 1)
                    dve.tensor_tensor(WV_l[:, :, D:D + 2], fold[:, 1, :, None].to_broadcast((P, DC, 2)),
                                      WV_h[:, :, D:D + 2].bitcast(F32), ALU.subtract).then_inc(qk_low, 1)
                elif kind in ("turn_w", "fold_w"):
                    n = t_use[st]
                    dve.wait_ge(t_high, t_use[st] + 1)
                    src = T_B[n % T_BANKS][:, :].rearrange("p (c e) -> p c e", c=DC)
                    if a == 3:
                        dve.wait_ge(gres_in, 16)
                        for c in range(DC):
                            i = dve.scalar_tensor_tensor(WT_l[:, 2, c, :], src[:, c, :], cols[:, 2, c:c + 1],
                                                         WT_h[:, 2, c, :].bitcast(F32), ALU.mult, ALU.subtract)
                        i.then_inc(t_freed, 1)
                    else:
                        low, high = (WV_l[:, :, 0:D], WV_h[:, :, 0:D]) if a == 2 else (WT_l[:, 0, :, :], WT_h[:, 0, :, :])
                        dve.tensor_tensor(low, src, high.bitcast(F32),
                                          ALU.subtract).then_inc(t_freed, 1)
                elif kind == "xstat":
                    dve.wait_ge(x_in[a // GROUP], 16)
                    row_stats(st, X[:, a, :], a)
                elif kind == "turn_x":
                    n = t_use[st]
                    dve.wait_ge(t_high, t_use[st] + 1)
                    dve.tensor_tensor(x_part(1, a)[:, b, :], T_B[n % T_BANKS][:, :],
                                      x_part(0, a)[:, b, :].bitcast(F32), ALU.subtract).then_inc(t_freed, 1)
                elif kind == "turn_p":
                    n, k, w = t_use[st], p_use[(a, b)] % PT_SLOTS, P * blocks_of(a, b)
                    dve.wait_ge(t_high, t_use[st] + 1)
                    dve.tensor_tensor(PT_l[:, k, 0:w], T_B[n % T_BANKS][:, 0:w],
                                      PT_h[:, k, 0:w].bitcast(F32), ALU.subtract).then_inc(t_freed, 1)
                elif kind == "proj":
                    n = s_use[st]
                    src = S_B[n % S_BANKS][:, :]
                    dve.wait_ge(s_high, high_no[st] + 1)
                    if b < 2:
                        dve.scalar_tensor_tensor(g_part(1, a)[:, b, :], src, fold[:, 0, b:b + 1],
                                                 g_part(0, a)[:, b, :].bitcast(F32), ALU.add,
                                                 ALU.subtract).then_inc(s_freed, 1)
                    else:
                        t = GROUP * a + b - 2
                        dve.wait_ge(fold_kept, 1)
                        dve.tensor_scalar(row_term[:, t:t + 1], src[:, D:D + 1], fold[:, 2, 0:1], fold[:, 2, 1:2],
                                          ALU.add, ALU.add)
                        dve.tensor_tensor(V[:, t, 1, :], src[:, 0:D], V[:, t, 0, :].bitcast(F32),
                                          ALU.subtract).then_inc(s_freed, 1)
                elif kind == "score":
                    n, w = s_use[st], P * blocks_of(a, b)
                    dve.wait_ge(s_filled, n + 1)
                    if a < 2:
                        dve.wait_ge(t_filled, t_use[("turn_w", 3, 0)] + 1)
                    if a >= 2:
                        dve.wait_ge(t_filled, t_use[("turn_p", a - 2, chunks_of(a - 2) - 1)] + 1)
                    dve.wait_ge(s_freed, s_use[("proj", a // GROUP, 2 + a % GROUP)] + 1)
                    dve.tensor_scalar(SC[:, a % 2, b * 512:b * 512 + w], S_B[n % S_BANKS][:, 0:w],
                                      row_term[:, a:a + 1], None, ALU.add, ALU.max,
                                      accum_out=cmax[:, a % 2, b:b + 1]).then_inc(s_freed, 1)
                elif kind == "top":
                    n = chunks_of(a)
                    dve.wait_ge(s_freed, s_use[("score", a, n - 1)] + 1)
                    if a >= 2:
                        dve.wait_ge(probs_ready, e_use[(a - 2, chunks_of(a - 2) - 1)] + 1)
                    dve.tensor_reduce(top[:, a % 2:a % 2 + 1], cmax[:, a % 2, 0:n], AX.X, ALU.max).then_inc(top_ready, 1)
                    dve.wait_ge(top_ready, a + 1)
                    dve.tensor_scalar(nmax[:, a % 2:a % 2 + 1], top[:, a % 2:a % 2 + 1], -SCALE, None,
                                      ALU.mult).then_inc(nmax_ready, 1)
                elif kind == "attn_out":
                    dve.wait_ge(pv_done, p_use[(a, chunks_of(a) - 1)] + 1)
                    dve.wait_ge(rl_ready, a + 1)
                    dve.wait_ge(xb_ready, a + 1)
                    dve.scalar_tensor_tensor(X[:, a, :], O_B[:, 0:D], rl[:, a % 2:a % 2 + 1], X[:, a, :],
                                             ALU.mult, ALU.add).then_inc(x1_ready, 1)
                    dve.wait_ge(x1_ready, a + 1)
                    row_stats(st, X[:, a, :], norm_cols(st).start)
                    if in_tail(st):
                        padded_var(dve, st, 1.0 + RMS_EPS, RMS_EPS * LN_EPS)
                elif kind == "y":
                    dve.wait_ge(rs_ready, norm_no[("attn_out", a, 0)] + 1)
                    if a == 0:
                        dve.wait_ge(table_stored, 32)
                    if a >= 2:
                        dve.wait_ge(yt_filled, a - 1)
                    normed(Y[:, a % 2, :], X[:, a, :], ("attn_out", a, 0), 0, y_ready)
                elif kind == "turn_y":
                    dve.wait_ge(yt_high, a + 1)
                    dve.tensor_tensor(YT_l[:, :, :], Y_B[:, 0:D].rearrange("p (c r) -> p c r", c=DC),
                                      YT_h[:, :, :].bitcast(F32), ALU.subtract).then_inc(yt_low, 1)
                    if a >= TILES - TAIL:
                        add_patches(dve, a)
                elif kind == "x2":
                    dve.wait_ge(h_done, a + 1)
                    dve.wait_ge(patches_added, a + 1)
                    dve.tensor_tensor(X[:, a, :], Y_B[:, 0:D], X[:, a, :], ALU.add).then_inc(x2_ready, 1)
                    dve.wait_ge(x2_ready, a + 1)
                    row_stats(st, X[:, a, :], norm_cols(st).start)
                    if in_tail(st):
                        padded_var(dve, st, 1.0, LN_EPS)
                elif kind == "z":
                    s = a % 2
                    dve.wait_ge(rs_ready, norm_no[("x2", a, 0)] + 1)
                    normed(Z[:, s, :], X[:, a, :], ("x2", a, 0), 0, z_ready)
                    dve.wait_ge(z_ready, a + 1)
                    if a >= TILES - TAIL:
                        dve.wait_ge(scl_ready, 2)
                        if a >= 2:
                            dve.wait_ge(q_ready, a - 1)
                        dve.tensor_scalar(VV[:, s, :], Z[:, s, :], scl[:, 2:3], None, ALU.mult).then_inc(v_ready, 1)
                    else:
                        greatest_z(a)
                elif kind == "bits":
                    s = a % 2
                    if a >= 2:
                        dve.wait_ge(q_ready, a - 1)
                    dve.wait_ge(v_ready, a + 1)
                    dve.tensor_scalar(MG[:, s, :].bitcast(I32), VV[:, s, :].bitcast(I32), 0x7F800000, None,
                                      ALU.bitwise_and).then_inc(bits_ready, 1)
                    if a < TILES - TAIL:
                        scaled_greatest_z(a)
                    dve.wait_ge(bits_ready, a + 1)
                    dve.tensor_scalar(MG[:, s, :], MG[:, s, :], 2.0 ** -6, 1.5 * 2.0 ** 20,
                                      ALU.max, ALU.mult).then_inc(magic_ready, 1)
                    if a >= TILES - TAIL:
                        round_rows(dve, a)
                        greatest_z(a)
                        scaled_greatest_z(a)
                    if a >= 2:
                        dve.wait_ge(f_ready, a - 1)
                    dve.wait_ge(z_scaled, a + 1)
                    dve.tensor_scalar(nanf[:, s, 0:1], zmax[:, s:s + 1], E4M3_MAX, 3.0e38, ALU.is_gt,
                                      ALU.mult).then_inc(nan_step, 1)
                    dve.wait_ge(nan_step, 2 * a + 1)
                    dve.tensor_scalar(nanf[:, s, 1:2], nanf[:, s, 0:1], 1.0e10, 0.0, ALU.mult,
                                      ALU.mult).then_inc(nan_step, 1)
                elif kind == "store" and a >= TILES - TAIL:
                    finish_rows(dve, a)
                elif kind == "quant_k" and b == 0:
                    dve.wait_ge(scl_in, 32)
                    dve.reciprocal(scl[:, 2:4], scl[:, 0:2]).then_inc(scl_ready, 1)
                    dve.tensor_tensor(ss[:, :], scl[:, 0:1], scl[:, 1:2], ALU.mult).then_inc(scl_ready, 1)
                    dve.wait_ge(kern_in, 16)
                    dve.wait_ge(scl_ready, 2)
                    dve.wait_ge(t_filled, t_use[("turn_w", 3, 0)] + 1)
                    dve.tensor_scalar(kv[:, :, :], kraw[:, :, :], scl[:, 3:4], None, ALU.mult).then_inc(kq_step, 1)
                    dve.wait_ge(kq_step, 1)
                    dve.tensor_scalar(km[:, :, :].bitcast(I32), kv[:, :, :].bitcast(I32), 0x7F800000, None,
                                      ALU.bitwise_and).then_inc(kq_step, 1)
                    dve.wait_ge(kq_step, 2)
                    dve.tensor_scalar(km[:, :, :], km[:, :, :], 2.0 ** -6, 1.5 * 2.0 ** 20, ALU.max,
                                      ALU.mult).then_inc(kq_step, 1)
                elif kind == "quant_k":
                    dve.wait_ge(kq_pool, 2)
                    dve.tensor_scalar(km[:, :, :], kv[:, :, :], 3.4028e38 / E4M3_MAX, None,
                                      ALU.mult).then_inc(kq_step, 1)
                    dve.wait_ge(kq_step, 4)
                    dve.tensor_tensor(km[:, :, :], km[:, :, :], km[:, :, :], ALU.subtract).then_inc(kq_step, 1)
                    dve.wait_ge(kq_step, 5)
                    dve.tensor_tensor(kq[:, :, :], kv[:, :, :], km[:, :, :], ALU.add).then_inc(kq_ready, 1)
                elif kind == "ends_limb":
                    dve.wait_ge(lens_in, 32)
                    dve.tensor_scalar(limb[:, 0, :], ln[:, :], 2047, None, ALU.bitwise_and).then_inc(limbs_cut, 1)
                    dve.tensor_scalar(limb[:, 1, :], ln[:, :], 11, 2047, ALU.logical_shift_right,
                                      ALU.bitwise_and).then_inc(limbs_cut, 1)
                    dve.tensor_scalar(limb[:, 2, :], ln[:, :], 22, 1023, ALU.logical_shift_right,
                                      ALU.bitwise_and).then_inc(limbs_cut, 1)
                    dve.wait_ge(limbs_cut, 3)
                    dve.tensor_copy(limf[:, :, :], limb[:, :, :]).then_inc(limbs_float, 1)
                    dve.wait_ge(limbs_float, 1)
                    dve.wait_ge(const_ready, 3)
                    for m in range(3):
                        dve.tensor_tensor_scan(limc[:, m, :], onef[:, 0:PER], limf[:, m, :], 0.0, ALU.mult,
                                               ALU.add).then_inc(limbs_run, 1)
                elif kind == "ends_sum":
                    dve.wait_ge(ends_pe, 1)
                    dve.tensor_copy(limp[:, :], Q_B[:, 0:3]).then_inc(limbs_before, 1)
                elif kind == "ends_int":
                    dve.wait_ge(limbs_run, 3)
                    dve.wait_ge(limbs_before, 1)
                    for m in range(3):
                        dve.tensor_scalar(limt[:, m, :], limc[:, m, :], limp[:, m:m + 1], -1.0 if m == 0 else 0.0,
                                          ALU.add, ALU.add).then_inc(limbs_whole, 1)
                    dve.wait_ge(limbs_whole, 3)
                    for m in range(1, 3):
                        dve.tensor_scalar(limt[:, m, :], limt[:, m, :], 11 * m, None,
                                          ALU.logical_shift_left).then_inc(limbs_shifted, 1)
                elif kind == "ends_place":
                    dve.wait_ge(ends_pool, 2)
                    dve.tensor_scalar(endi[:, 1, :], endi[:, 0, :], P - 1, None, ALU.bitwise_and).then_inc(ends_split, 1)
                    dve.tensor_scalar(endi[:, 2, :], endi[:, 0, :], int(math.log2(P)), TILES - 1,
                                      ALU.logical_shift_right, ALU.bitwise_and).then_inc(ends_split, 1)
                    dve.wait_ge(ends_split, 2)
                    dve.tensor_copy(endf[:, 0:3, :], endi[:, 0:3, :]).then_inc(ends_float, 1)
                    dve.wait_ge(ends_float, 1)
                    dve.tensor_scalar(endf[:, 3, :], endf[:, 0, :], float(S - 1), 100.0, ALU.is_gt,
                                      ALU.mult).then_inc(ends_outside, 1)
                    dve.tensor_scalar(endf[:, 0, :], endf[:, 0, :], float(-S), 100.0, ALU.is_lt,
                                      ALU.mult).then_inc(ends_outside, 1)
                    dve.wait_ge(ends_outside, 2)
                    dve.tensor_tensor(endf[:, 2, :], endf[:, 2, :], endf[:, 3, :], ALU.add).then_inc(ends_kept, 1)
                    dve.wait_ge(ends_kept, 1)
                    dve.tensor_tensor(endf[:, 2, :], endf[:, 2, :], endf[:, 0, :], ALU.add).then_inc(ends_kept, 1)
                elif kind == "ends_hot":
                    dve.wait_ge(const_ready, 10)
                    ks = slice(0, PER // 2) if b == 0 else slice(PER // 2, PER)
                    n = ks.stop - ks.start
                    dve.tensor_tensor(hot_lo[:, ks, :], iota[:, None, :].to_broadcast((P, n, P)),
                                      endf[:, 1, ks, None].to_broadcast((P, n, P)), ALU.is_equal).then_inc(hot_ready, 1)
                    if b == 1:
                        dve.wait_ge(ends_kept, 2)
                        dve.tensor_tensor(hot_hi[:, :, :], iota[:, None, 0:TILES].to_broadcast((P, PER, TILES)),
                                          endf[:, 2, :, None].to_broadcast((P, PER, TILES)),
                                          ALU.is_equal).then_inc(hot_ready, 1)
                elif kind == "ends_mask":
                    dve.wait_ge(ends_pe, 2)
                    dve.tensor_scalar(bmask[:, :], Q_B[:, 0:TILES], 1.0, None, ALU.min).then_inc(bmask_ready, 1)
                elif kind == "ends_rank":
                    dve.wait_ge(ends_pe, 3)
                    dve.tensor_copy(btot[:, 0:2, :], Q_B[:, 0:2 * TILES].rearrange("p (a t) -> p a t", a=2)).then_inc(btot_ready, 1)
                elif kind == "ends_index":
                    dve.wait_ge(btot_ready, 1)
                    dve.tensor_tensor_scan(btot[:, 2, :], onef[:, 0:TILES], btot[:, 1, :], 0.0, ALU.mult,
                                           ALU.add).then_inc(brun_ready, 1)
                    dve.tensor_tensor(btot[:, 3, :], btot[:, 0, :], btot[:, 1, :], ALU.subtract).then_inc(brun_ready, 1)
                    dve.wait_ge(brun_ready, 2)
                    dve.scalar_tensor_tensor(btot[:, 0, :], btot[:, 2, :], -1.0, btot[:, 3, :], ALU.add,
                                             ALU.add).then_inc(rank_ready, 1)
                    dve.wait_ge(rank_ready, 1)
                    dve.tensor_scalar(plug[:, :], btot[:, 0, :], 0.0, float(NPATCH - 1), ALU.max,
                                      ALU.min).then_inc(plug_ready, 1)
                elif kind == "run" and b >= 1:
                    dve.wait_ge(patch_u, b + 1)
                    if b >= 2:
                        dve.wait_ge(patch_run, b - 1)
                    dve.scalar_tensor_tensor(CT[0:PP, b, 0:D], CT[0:PP, b - 1, 0:D], PATCH_A, CT[0:PP, b, 0:D],
                                             ALU.mult, ALU.add).then_inc(patch_run, 1)
                elif kind == "fix":
                    dve.wait_ge(carry_ready, 1)
                    dve.wait_ge(patch_run, PER - 1)
                    dve.scalar_tensor_tensor(CT[0:PP, b, 0:D], carry[0:PP, :], PATCH_A ** (b + 1),
                                             CT[0:PP, b, 0:D], ALU.mult, ALU.add).then_inc(patch_fixed, 1)
                elif kind == "pv" and b == chunks_of(a) - 1:
                    dve.wait_ge(probs_ready, e_use[(a, b)] + 1)
                    dve.tensor_reduce(lall[:, a % 2:a % 2 + 1], lsum[:, a % 2, 0:b + 1], AX.X, ALU.add).then_inc(lall_ready, 1)
                    dve.wait_ge(lall_ready, a + 1)
                    dve.reciprocal(rl[:, a % 2:a % 2 + 1], lall[:, a % 2:a % 2 + 1]).then_inc(rl_ready, 1)


_INS = ["x", "ctx_2048", "mask_BxS2_if0", "L0_attn_Wq", "L0_attn_bq", "L0_attn_Wk", "L0_attn_bk",
        "L0_attn_Wv", "L0_attn_bv", "L0_xattn_W_in", "L0_xattn_b_in", "L0_xattn_g_res", "L0_xattn_g_init",
        "L0_ffn_kernel", "L0_ffn_input_scale", "L0_ffn_kernel_scale", "L0_ffn_bias"]


def kernel(**inputs):
    import numpy as _np
    import concourse.bacc as _bacc
    from concourse import mybir as _mybir
    from concourse.bass_utils import run_bass_kernel_spmd as _run

    nc = _bacc.Bacc("TRN2", target_bir_lowering=False, num_devices=1)
    arrays, args = {}, []
    for name in _INS:
        a = _np.ascontiguousarray(inputs[name])
        arrays[f"in_{name}_dram"] = a
        args.append(nc.dram_tensor(f"in_{name}_dram", a.shape, _mybir.dt.from_np(a.dtype), kind="ExternalInput").ap())
    patches = inputs["ctx_2048"].shape[1]
    rows = inputs["x"].shape
    args.append(nc.dram_tensor("patch_table", (patches, rows[2]), F32, kind="Internal").ap())
    args.append(nc.dram_tensor("out_0_dram", rows, F32, kind="ExternalOutput").ap())
    decoder_layer(nc, *args)
    r = _run(nc, [arrays], core_ids=[0])
    return r.results[0]["out_0_dram"]
```
